# Optimizing a Trainium2 kernel written in Bass

```python
import numpy as np
import jax
import jax.numpy as jnp

def _softmax(x, axis=-1):
    return jax.nn.softmax(x, axis=axis)
def _gelu(x):
    return jax.nn.gelu(x, approximate=True)
def _silu(x):
    return jax.nn.silu(x)
def _sigmoid(x):
    return jax.nn.sigmoid(x)
def _layernorm(x, axis=-1, eps=1e-5):
    m = jnp.mean(x, axis=axis, keepdims=True)
    v = jnp.var(x, axis=axis, keepdims=True)
    return (x - m) / jnp.sqrt(v + eps)
def _scatter_add(tgt, idx, src, axis=0):
    return tgt.at[idx].add(src)
def _segment_sum(src, seg, n):
    return jax.ops.segment_sum(src, seg, n)

kernel_name = 'mk_conv_preact_d1_conv_nchw96_1f175a'

def setup_inputs(seed: int = 0):
    np.random.seed(seed)
    _w = jnp.asarray
    def _rec_inputs():
        import jax
        import jax.numpy as jnp
        _gk = jax.random.key(seed)
        x = -0.0002221 + 1 * jax.random.normal(jax.random.fold_in(_gk, 1), (4, 96, 256, 256), jnp.float32)
        return x
    x = _rec_inputs()
    def _L0_conv_setup():
        import jax, jax.numpy as jnp
        import numpy as np
        from jax import lax
        DIM = 96
        HID = int(DIM * 2.0)
        C2 = HID * 2
        P = 8
        B, H, W = (4, 256, 256)

        def _dwconv(x, w):
            return lax.conv_general_dilated(x, w, window_strides=(1, 1), padding='SAME', feature_group_count=x.shape[1], dimension_numbers=('NCHW', 'OIHW', 'NCHW'))
        key = jax.random.key(seed)
        ks = jax.random.split(key, 7)
        x = jax.random.normal(ks[0], (B, DIM, H, W), dtype=jnp.float32)
        w_in = jax.random.normal(ks[1], (C2, DIM), dtype=jnp.float32) * (1.0 / np.sqrt(DIM))
        w_dw = jax.random.normal(ks[2], (C2, 1, 3, 3), dtype=jnp.float32) * (1.0 / 3.0)
        w_dw3 = jax.random.normal(ks[3], (HID, 1, 3, 3), dtype=jnp.float32) * (1.0 / 3.0)
        w_dw5 = jax.random.normal(ks[4], (HID, 1, 5, 5), dtype=jnp.float32) * (1.0 / 5.0)
        fft_filt = jnp.ones((C2, 1, 1, P, P // 2 + 1), dtype=jnp.float32)
        w_out = jax.random.normal(ks[5], (DIM, HID), dtype=jnp.float32) * (1.0 / np.sqrt(HID))
        return {'x': x, 'w_in': w_in, 'w_dw': w_dw, 'w_dw3': w_dw3, 'w_dw5': w_dw5, 'fft_filt': fft_filt, 'w_out': w_out}
    _L0_conv_all = _L0_conv_setup()
    _L0_conv_in = {k: v for k, v in _L0_conv_all.items() if k in ('w_in', 'w_dw', 'w_dw3', 'w_dw5', 'fft_filt', 'w_out', )}
    del _L0_conv_all

    return {
        "x": x,
        "L0_conv_w_in": _L0_conv_in["w_in"],
        "L0_conv_w_dw": _L0_conv_in["w_dw"],
        "L0_conv_w_dw3": _L0_conv_in["w_dw3"],
        "L0_conv_w_dw5": _L0_conv_in["w_dw5"],
        "L0_conv_fft_filt": _L0_conv_in["fft_filt"],
        "L0_conv_w_out": _L0_conv_in["w_out"],
    }

def reference(x, L0_conv_w_in, L0_conv_w_dw, L0_conv_w_dw3, L0_conv_w_dw5, L0_conv_fft_filt, L0_conv_w_out):
    import jax
    import jax.numpy as jnp
    def _L0_conv_ref(x, w_in, w_dw, w_dw3, w_dw5, fft_filt, w_out):
        import jax, jax.numpy as jnp
        import numpy as np
        from jax import lax
        DIM = 96
        HID = int(DIM * 2.0)
        C2 = HID * 2
        P = 8
        B, H, W = (4, 256, 256)

        def _dwconv(x, w):
            return lax.conv_general_dilated(x, w, window_strides=(1, 1), padding='SAME', feature_group_count=x.shape[1], dimension_numbers=('NCHW', 'OIHW', 'NCHW'))
        b, _, h, w = x.shape
        x = jnp.einsum('oc,bchw->bohw', w_in, x)
        xp = x.reshape(b, C2, h // P, P, w // P, P).transpose(0, 1, 2, 4, 3, 5)
        xf = jnp.fft.rfft2(xp.astype(jnp.float32))
        xf = xf * fft_filt
        xp = jnp.fft.irfft2(xf, s=(P, P))
        x = xp.transpose(0, 1, 2, 4, 3, 5).reshape(b, C2, h, w)
        x12 = _dwconv(x, w_dw)
        x1, x2 = (x12[:, :HID], x12[:, HID:])
        x1_3 = jax.nn.relu(_dwconv(x1, w_dw3))
        x2_5 = jax.nn.relu(_dwconv(x2, w_dw5))
        x = jax.nn.gelu(x1_3, approximate=False) * x2_5
        return jnp.einsum('oc,bchw->bohw', w_out, x)

    def _gn(v, G=32, eps=1e-5):
        B_, C_, H_, W_ = v.shape
        g = v.reshape(B_, G, C_ // G, H_, W_)
        m = jnp.mean(g, axis=(2, 3, 4), keepdims=True)
        s = jnp.var(g, axis=(2, 3, 4), keepdims=True)
        return ((g - m) / jnp.sqrt(s + eps)).reshape(v.shape)

    def _ln_c(v, eps=1e-6):
        m = jnp.mean(v, axis=1, keepdims=True)
        s = jnp.var(v, axis=1, keepdims=True)
        return (v - m) / jnp.sqrt(s + eps)

    def _ln_t(v, eps=1e-5):
        m = jnp.mean(v, axis=-1, keepdims=True)
        s = jnp.var(v, axis=-1, keepdims=True)
        return (v - m) / jnp.sqrt(s + eps)

    def _to_tokens(v):
        B_, C_, H_, W_ = v.shape
        return v.reshape(B_, C_, H_ * W_).transpose(0, 2, 1)
    def _from_tokens(t, like):
        B_, C_, H_, W_ = like.shape
        return t.transpose(0, 2, 1).reshape(B_, C_, H_, W_)

    x = x + _L0_conv_ref(_gn(x), L0_conv_w_in, L0_conv_w_dw, L0_conv_w_dw3, L0_conv_w_dw5, L0_conv_fft_filt, L0_conv_w_out)
    return x


_drawn_inputs = setup_inputs


def setup_inputs(seed=0):
    import zlib

    import numpy as np

    out = dict(_drawn_inputs(seed))
    spreads = {'L0_conv_fft_filt': (1.0, 0.2)}
    factors = {}
    for name, (base, spread) in spreads.items():
        noise = np.random.default_rng([zlib.crc32(name.encode()), seed]).standard_normal(out[name].shape)
        drawn = base * np.exp(spread * noise) if base else spread * noise
        out[name] = jnp.asarray(drawn.astype(out[name].dtype))
    for name, factor in factors.items():
        out[name] = (out[name] * factor).astype(out[name].dtype)
    return out
```

```python
from contextlib import ExitStack

import concourse.bass as bass
from concourse import mybir

F32 = mybir.dt.float32
ALU = mybir.AluOpType
AF = mybir.ActivationFunctionType

B, DIM, H, W = 4, 96, 256, 256
HID = 2 * DIM
C2 = 2 * HID
PIX = H * W
P8 = 8
BR = H // P8
MC = W // P8
TJ = W // 16
OFF = 3
ROWPIX = P8 * W
CT = C2 // 128
TROW = 40
ZT = 16
TAB = ZT * 2 * P8 * TROW
WIN = 2 * P8 * TROW - 8
XTAB = ZT * 2 * P8 * 4
KTAB = 15 * 16
KWIN = 7 * 16 + 8
NE = 11
TILES = B * BR * TJ
EPS = 1e-5
EDGE = [(0, 4), (0, 3), (2, 1), (2, 0)]


def wait(eng, sem, value):
    if not isinstance(value, int) or value > 0:
        eng.wait_ge(sem, value)


def over(eng, n, body):
    body(0)
    with eng.Fori(1, n) as i:
        body(i)


def dram(tensor, offset, dims):
    return bass.AP(tensor.tensor, offset, dims)


def stage_a(nc, io, keep, scratch):
    CH = 2048
    NCH = PIX // CH
    RING = 4
    with ExitStack() as ctx:
        sb = lambda name, shape: ctx.enter_context(nc.sbuf_tensor(name, shape, F32))
        sem = lambda name: ctx.enter_context(nc.semaphore(name))
        ps = ctx.enter_context(nc.psum_tensor("psA", [128, 8, 512], F32))
        xs = sb("xsA", [DIM, RING, CH])
        stats = sb("stats", [DIM, NCH * CH // 512, 6])
        mv = sb("mv", [DIM, B, 2])
        small = sb("small", [DIM, 10, B])
        win = sb("win", [128, CT, DIM])
        wout = sb("wout", [DIM, HID])
        filt = sb("filt", [128, CT, 40])
        filtT = sb("filtT", [40, C2])
        dft = sb("dft", [40, KTAB])
        group = sb("group", [DIM, DIM])
        kper = sb("kper", [128, CT, KTAB])
        w1 = sb("w1", [128, CT, 9])
        w2 = sb("w2", [128, CT, 25])
        prod = sb("prod", [128, CT, 3, 5])
        h = sb("h", [128, NE, CT, 3, 5])
        cf = sb("cf", [128, CT, 7, NE])
        tab = sb("tab", [128, CT, ZT, 2, P8, TROW])
        xtab = sb("xtab", [128, CT, ZT, 2, P8, 4])
        x_in = [sem(f"x_in{k}") for k in range(RING)]
        x_used = sem("x_used")
        params = sem("params")
        w2_clear = sem("w2_clear")
        w2_in = sem("w2_in")
        turned = sem("turned")
        turned_sb = sem("turned_sb")
        kper_ps = sem("kper_ps")
        kper_sb = sem("kper_sb")
        aggr = sem("aggr")
        seg = sem("seg")
        g_mean = sem("g_mean")
        g_in = sem("g_in")
        g_var = sem("g_var")
        var_eps = sem("var_eps")
        root = sem("root")
        vchain = sem("vchain")
        pchain = sem("pchain")
        tab_ready = sem("tab_ready")
        tab_out = sem("tab_out")
        kper_out = sem("kper_out")
        NPAR = 4 + 4 + 3 + 1
        block = ctx.enter_context(nc.Block())

        @block.sync
        def _(sp):
            for dst, src in ((keep["ident"][:], io["ident"]), (keep["mask"][:], io["mask"]), (keep["xmask"][:], io["xmask"]),
                             (dft[:], io["dft"]), (group[:], io["group"]), (wout[:], io["w_out"]),
                             (win[:], io["w_in"].rearrange("(t p) c -> p t c", p=128)),
                             (filt[:], io["filt"].rearrange("(t p) a b u v -> p t (a b u v)", p=128)),
                             (w1[:], io["w_dw"].rearrange("(t p) a u v -> p t (a u v)", p=128))):
                sp.dma_start(dst, src).then_inc(params, 16)
            sp.wait_ge(w2_clear, 1)
            w3 = io["w_dw3"].rearrange("o a u v -> o (a u) v")
            w5 = io["w_dw5"].rearrange("o a u v -> o (a u v)")
            mid = w2[:].rearrange("p t (u v) -> p t u v", u=5)[:, :, 1:4, 1:4]
            sp.dma_start(mid[:, 0], w3[0:128]).then_inc(w2_in, 16)
            sp.dma_start(mid[0:64, 1], w3[128:192]).then_inc(w2_in, 16)
            sp.dma_start(w2[64:128, 1], w5[0:64]).then_inc(w2_in, 16)
            sp.dma_start(w2[:, 2], w5[64:192]).then_inc(w2_in, 16)

            def load(img, q):
                for k in range(RING):
                    n = img * (NCH) + q * RING + k
                    wait(sp, x_used, n - (RING - 1))
                    sp.dma_start(xs[:, k], dram(io["x"], img * (DIM * PIX) + (q * RING + k) * CH, [[PIX, DIM], [1, CH]])
                                 ).then_inc(x_in[k], 16)
            for img in range(B):
                over(sp, NCH // RING, lambda q, img=img: load(img, q))

        @block.vector
        def _(v):
            def chain(ins):
                chain.n += 1
                ins.then_inc(vchain, 1)
                v.wait_ge(vchain, chain.n)
            chain.n = 0
            v.memset(w2[:], 0.0).then_inc(w2_clear, 1)

            def chunk_stats(img, q):
                for k in range(RING):
                    v.wait_ge(x_in[k], (img * (NCH // RING) + q + 1) * 16)
                    for j in range(CH // 512):
                        at = (q * RING + k) * (CH // 512) + j
                        ins = v.bn_stats(stats[:, at, :] if isinstance(at, int) else stats[:, bass.ds(at, 1), :],
                                         xs[:, k, j * 512:(j + 1) * 512])
                    ins.then_inc(x_used, 1)
            for img in range(B):
                if img:
                    v.wait_ge(aggr, img)
                over(v, NCH // RING, lambda q, img=img: chunk_stats(img, q))
                v.wait_ge(x_used, NCH * (img + 1))
                v.bn_aggr(mv[:, img, :], stats[:].rearrange("p a b -> p (a b)")).then_inc(aggr, 1)
            mg, dev, dv2, vin, ve, sd, r, t1, t2, t3 = (small[:, k, :] for k in range(10))
            v.wait_ge(g_mean, 1)
            chain(v.tensor_copy(mg, ps[0:DIM, 5, 0:B]))
            chain(v.tensor_tensor(dev, mv[:, :, 0], mg, ALU.subtract))
            chain(v.tensor_tensor(dv2, dev, dev, ALU.mult))
            v.tensor_tensor(vin, dv2, mv[:, :, 1], ALU.add).then_inc(g_in, 1)
            v.wait_ge(g_var, 1)
            v.tensor_scalar(ve, ps[0:DIM, 6, 0:B], EPS, None, ALU.add).then_inc(var_eps, 1)
            v.wait_ge(root, 1)
            chain(v.reciprocal(r, sd))
            v.wait_ge(var_eps, 1)
            chain(v.tensor_tensor(t1, r, r, ALU.mult))
            chain(v.tensor_tensor(t2, t1, ve, ALU.mult))
            chain(v.tensor_scalar(t3, t2, -0.5, 1.5, ALU.mult, ALU.add))
            chain(v.tensor_tensor(keep["scale"][:], r, t3, ALU.mult))
            chain(v.tensor_tensor(dev, mg, keep["scale"][:], ALU.mult))
            v.tensor_scalar(keep["shift"][:], dev, -1.0, None, ALU.mult)

        @block.tensor
        def _(pe):
            pe.wait_ge(params, 16 * 9)
            ident = keep["ident"]
            for t in range(CT):
                pe.transpose(ps[0:DIM, 0, t * 128:(t + 1) * 128], win[:, t, :], ident[:])
            for t in range(CT):
                pe.transpose(ps[0:40, 1, t * 128:(t + 1) * 128], filt[:, t, :], ident[:])
            for t in range(2):
                ins = pe.transpose(ps[0:DIM, 2, t * DIM:(t + 1) * DIM], wout[:, t * DIM:(t + 1) * DIM], ident[0:DIM, 0:DIM])
            ins.then_inc(turned, 1)
            pe.wait_ge(turned_sb, 1)
            for t in range(CT):
                ins = pe.matmul(ps[:, 3 + t // 2, (t % 2) * KTAB:(t % 2 + 1) * KTAB], filtT[:, t * 128:(t + 1) * 128], dft[:],
                                start=True, stop=True)
            ins.then_inc(kper_ps, 1)
            pe.wait_ge(aggr, B)
            pe.matmul(ps[0:DIM, 5, 0:B], group[:], mv[:, :, 0], start=True, stop=True).then_inc(g_mean, 1)
            pe.wait_ge(g_in, 1)
            pe.matmul(ps[0:DIM, 6, 0:B], group[:], small[:, 3, :], start=True, stop=True).then_inc(g_var, 1)

        @block.scalar
        def _(act):
            act.wait_ge(turned, 1)
            act.copy(filtT[:], ps[0:40, 1, 0:C2]).then_inc(turned_sb, 1)
            act.copy(keep["w_inT"][:], ps[0:DIM, 0, 0:C2])
            act.copy(keep["w_outT"][:].rearrange("p a b -> p (a b)"), ps[0:DIM, 2, 0:2 * DIM])
            act.wait_ge(kper_ps, 1)
            act.copy(kper[:, 0:2].rearrange("p a b -> p (a b)"), ps[:, 3, 0:2 * KTAB]).then_inc(kper_sb, 1)
            act.copy(kper[:, 2], ps[:, 4, 0:KTAB]).then_inc(kper_sb, 1)
            act.wait_ge(kper_sb, 2)
            act.dma_start(scratch["kper"].rearrange("(t p) k -> p t k", p=128), kper[:]).then_inc(kper_out, 16)
            act.wait_ge(tab_ready, 1)
            for t in range(CT):
                act.dma_start(scratch["tab"][t * 128:(t + 1) * 128], tab[:, t].rearrange("p a b c d -> p (a b c d)")).then_inc(tab_out, 16)
                act.dma_start(scratch["xtab"][t * 128:(t + 1) * 128], xtab[:, t].rearrange("p a b c d -> p (a b c d)")).then_inc(tab_out, 16)
            act.wait_ge(var_eps, 1)
            act.activation(small[:, 5, :], small[:, 4, :], AF.Sqrt).then_inc(root, 1)
            act.wait_ge(kper_out, 16)
            act.wait_ge(tab_out, 32 * CT)

        @block.gpsimd
        def _(pool):
            def chain(ins):
                chain.n += 1
                ins.then_inc(pchain, 1)
                pool.wait_ge(pchain, chain.n)
            chain.n = 0
            pool.memset(tab[:], 0.0)
            pool.memset(xtab[:], 0.0)
            chain(pool.memset(h[:], 0.0))
            pool.wait_ge(params, 16 * 9)
            pool.wait_ge(w2_in, 64)
            w1v = w1[:].rearrange("p t (a b) -> p t a b", a=3)
            w2v = w2[:].rearrange("p t (a b) -> p t a b", a=5)

            def rows_outer(ac, bc):
                chain(pool.tensor_tensor(prod[:], w1v[:, :, :, ac:ac + 1].broadcast_to([128, CT, 3, 5]),
                                         w2v[:, :, :, bc].unsqueeze(2).broadcast_to([128, CT, 3, 5]), ALU.mult))
            for ac in range(3):
                for bc in range(5):
                    rows_outer(ac, bc)
                    e = 6 - ac - bc
                    chain(pool.tensor_tensor(h[:, e], h[:, e], prod[:], ALU.add))
            for k, (ac, bc) in enumerate(EDGE):
                rows_outer(ac, bc)
                chain(pool.tensor_copy(h[:, 7 + k], prod[:]))
            chain(pool.memset(cf[:], 0.0))
            for a in range(3):
                for t in range(CT):
                    dst = cf[:, t, a:a + 5, :]
                    ins = pool.tensor_tensor(dst, dst, h[:, :, t, a, :].rearrange("p e b -> p b e"), ALU.add)
                chain(ins) if a == 2 else chain(ins)
            for z in range(ZT):
                zt = 7 - z if z < 8 else 23 - z
                for p in range(P8):
                    d = z - p
                    if not 0 <= d <= 6:
                        continue
                    for r in range(2):
                        if r == 1 and (z < 8) != (p + OFF < 8):
                            continue
                        pool.tensor_copy(tab[:, :, zt, r, p, 17:24], cf[:, :, d, 0:7])
                        ins = pool.tensor_copy(xtab[:, :, zt, r, p, :], cf[:, :, d, 7:NE])
            chain(ins)
            for z, p, a, b in ((7, 3, 0, 4), (7, 4, 0, 3), (8, 5, 2, 1), (8, 6, 2, 0)):
                zt = 7 - z if z < 8 else 23 - z
                for dst, e0, e1 in ((tab[:, :, zt, 1, p, 17:24], 0, 7), (xtab[:, :, zt, 1, p, :], 7, NE)):
                    ins = pool.tensor_tensor(dst, dst, h[:, e0:e1, :, a, b].rearrange("p e t -> p t e"), ALU.subtract)
            ins.then_inc(tab_ready, 1)


def stage_b(nc, io, keep, scratch):
    U = 4
    with ExitStack() as ctx:
        sb = lambda name, shape: ctx.enter_context(nc.sbuf_tensor(name, shape, F32))
        sem = lambda name: ctx.enter_context(nc.semaphore(name))
        ps = ctx.enter_context(nc.psum_tensor("psB", [128, 4, 1024], F32))
        xs = sb("xsB", [DIM, U, ROWPIX])
        xn = sb("xn", [DIM, 2, ROWPIX])
        y = sb("y", [128, 2, CT, ROWPIX])
        x_in = [sem(f"xb_in{k}") for k in range(U)]
        normed = sem("normed")
        scaled = sem("scaled")
        mm = sem("mm")
        by_dve = sem("by_dve")
        by_act = sem("by_act")
        stored = [sem(f"y_stored{k}") for k in range(2)]
        wrapped = sem("wrapped")
        block = ctx.enter_context(nc.Block())
        each = lambda eng, strip: [over(eng, BR // U, lambda i, img=img: [strip(img, U * i + k, k) for k in range(U)])
                                   for img in range(B)]
        halves = ((0, 0, 128, scratch["y"][0], 0), (1, 0, 64, scratch["y"][0], 128), (1, 64, 128, scratch["y"][1], 0),
                  (2, 0, 128, scratch["y"][1], 64))
        CHS = B * (BR + 1) * ROWPIX

        @block.sync
        def _(sp):
            def load(img, br, k):
                g = BR * img + br
                wait(sp, normed, g - (U - 1))
                sp.dma_start(xs[:, k], dram(io["x"], img * (DIM * PIX) + br * ROWPIX, [[PIX, DIM], [1, ROWPIX]])).then_inc(x_in[k], 16)
            each(sp, load)

        @block.gpsimd
        def _(pool):
            def norm(img, br, k):
                g = BR * img + br
                pool.wait_ge(x_in[k], ((BR * img + br - k) // U + 1) * 16 if isinstance(br, int) else (BR // U) * 16 * img + (br - k) * (16 // U) + 16)
                wait(pool, mm, 6 * (g - 1))
                pool.tensor_tensor(xn[:, k % 2], xs[:, k], keep["scale"][:, img:img + 1].broadcast_to([DIM, ROWPIX]), ALU.mult
                                   ).then_inc(scaled, 1)
                pool.wait_ge(scaled, g + 1)
                pool.tensor_tensor(xn[:, k % 2], xn[:, k % 2], keep["shift"][:, img:img + 1].broadcast_to([DIM, ROWPIX]), ALU.add
                                   ).then_inc(normed, 1)
            each(pool, norm)

        @block.tensor
        def _(pe):
            def strip(img, br, k):
                g = BR * img + br
                pe.wait_ge(normed, g + 1)
                for n in range(6):
                    slot = (6 * k + n) % 4
                    if n in (0, 1):
                        wait(pe, by_dve, 4 * g - 1 + n)
                    elif n in (2, 3):
                        wait(pe, by_act, 2 * g - 3 + n)
                    else:
                        wait(pe, by_dve, 4 * g - 3 + n)
                    for c in range(2):
                        ins = pe.matmul(ps[:, slot, c * 512:(c + 1) * 512], keep["w_inT"][:, (n // 2) * 128:(n // 2 + 1) * 128],
                                        xn[:, k % 2, (n % 2) * 1024 + c * 512:(n % 2) * 1024 + (c + 1) * 512], start=True, stop=True)
                    ins.then_inc(mm, 1)
            each(pe, strip)

        def copy_out(eng, copy, done, img, br, k, ns):
            g = BR * img + br
            h = (BR // 2) * img + (br - k) * 1 // 2 + k // 2 if isinstance(br, int) else None
            if h is None:
                wait(eng, stored[k % 2], (BR // 2) * 64 * img + (br - k) * 32 + (k // 2) * 64)
            else:
                wait(eng, stored[k % 2], 64 * h)
            for n in ns:
                eng.wait_ge(mm, 6 * g + n + 1)
                copy(y[:, k % 2, n // 2, (n % 2) * 1024:(n % 2 + 1) * 1024].rearrange("p (r c m) -> p r c m", r=4, c=8),
                     ps[:, (6 * k + n) % 4, :].rearrange("p (r m c) -> p r c m", r=4, c=8)).then_inc(done, 1)

        @block.vector
        def _(v):
            each(v, lambda img, br, k: copy_out(v, v.tensor_copy, by_dve, img, br, k, range(4)))

        @block.scalar
        def _(act):
            def strip(img, br, k):
                g = BR * img + br
                copy_out(act, act.copy, by_act, img, br, k, (4, 5))
                act.wait_ge(by_act, 2 * g + 2)
                act.wait_ge(by_dve, 4 * g + 4)
                for t, p0, p1, dst, c0 in halves:
                    act.dma_start(dram(dst, c0 * CHS + img * ((BR + 1) * ROWPIX) + br * ROWPIX, [[CHS, p1 - p0], [1, ROWPIX]]),
                                  y[p0:p1, k % 2, t, :]).then_inc(stored[k % 2], 16)

            each(act, strip)
            for k in range(2):
                act.wait_ge(stored[k], 64 * B * BR // 2)
            for dst in scratch["y"]:
                for img in range(B):
                    at = img * (BR + 1) * ROWPIX
                    act.dma_start(dram(dst, at + BR * ROWPIX, [[CHS, HID], [1, ROWPIX]]), dram(dst, at, [[CHS, HID], [1, ROWPIX]])
                                  ).then_inc(wrapped, 16)
            act.wait_ge(wrapped, 2 * B * 16)


def stage_c(nc, keep, scratch):
    NB = 5
    IN = B * 4 * (BR - 1)
    with ExitStack() as ctx:
        sb = lambda name, shape: ctx.enter_context(nc.sbuf_tensor(name, shape, F32))
        sem = lambda name: ctx.enter_context(nc.semaphore(name))
        ps = ctx.enter_context(nc.psum_tensor("psC", [128, 8, 512], F32))
        PT, PB, PM = 0, 2, 3
        d = sb("d", [128, 2, 2 * ROWPIX])
        win = sb("win_c", [128, 2, 2, P8, TROW])
        xwin = sb("xwin", [128, 2, 2, P8, 4])
        fwin = sb("fwin", [128, 2, KWIN])
        filt = sb("filt_c", [128, 2, 128])
        edge = sb("edge", [128, 2, 2, 3, P8, 16])
        yt = sb("yt", [128, 2, MC + 1, B, BR])
        mat = sb("mat", [128, 2, 4, 3, 128])
        g1 = sb("g1", [128, 4, IN])
        g1w = sb("g1w", [128, 64])
        zero = sb("zero", [128, 1])
        held = sb("held", [128, NB])
        gt = sb("gt", [128, 4, 16, BR])
        d_in = [sem(f"d_in{s}") for s in range(2)]
        win_in = [sem(f"win_in{s}") for s in range(2)]
        clear = sem("clear")
        turned = sem("turned_c")
        yt_set = [sem("yt_act"), sem("yt_dve")]
        edge_mul = sem("edge_mul")
        edge_set = sem("edge_set")
        filt_set = sem("filt_set")
        built = sem("built")
        mat_set = sem("mat_set")
        prod = sem("prod_c")
        gelu_set = sem("gelu_set")
        clipped = sem("clipped")
        gated = sem("gated")
        g_out = sem("g_out")
        block = ctx.enter_context(nc.Block())
        CHS = B * (BR + 1) * ROWPIX

        def tasks(eng, prepare, run):
            def pair(t, last=False):
                run(t, 0, t, 1)
                run(t, 1, None if last else t + 1, 0)
            prepare()
            pair(0)
            with eng.Fori(1, HID - 1) as t:
                pair(t)
            pair(HID - 1, True)

        @block.sync
        def _(sp):
            sp.wait_ge(clear, 1)

            def load(t, s):
                u = 2 * t + s
                ys = scratch["y"][s]
                wait(sp, turned, 8 * (u - 1))
                for img in range(B):
                    sp.dma_start(d[img * BR:(img + 1) * BR, s],
                                 dram(ys, t * CHS + img * ((BR + 1) * ROWPIX), [[ROWPIX, BR], [1, 2 * ROWPIX]])).then_inc(d_in[s], 16)
                wait(sp, built, 4 * (u - 1))
                c = t + s * HID
                sp.dma_start(win[:, s].rearrange("p a b c -> p (a b c)")[:, 0:WIN],
                             dram(scratch["tab"], c * TAB, [[2 * P8 * TROW, ZT], [1, 8], [1, WIN]])).then_inc(win_in[s], 16)
                sp.dma_start(xwin[:, s].rearrange("p a b c -> p (a b c)"),
                             dram(scratch["xtab"], c * XTAB, [[64, ZT], [0, 8], [1, 64]])).then_inc(win_in[s], 16)
                for r in range(2):
                    sp.dma_start(fwin[64 * r:64 * r + 64, s],
                                 dram(scratch["kper"], c * KTAB, [[16, 8], [1, 8], [1, KWIN]])).then_inc(win_in[s], 16)

            load(0, 0)
            load(0, 1)
            with sp.Fori(1, HID) as t:
                load(t, 0)
                load(t, 1)

        @block.tensor
        def _(pe):
            ident = keep["ident"]

            def turn(t, s, j):
                u = 2 * t + s
                if j == 0:
                    pe.wait_ge(d_in[s], 64 * (t + 1))
                wait(pe, yt_set[j % 2], 4 * u + j // 2)
                for m in range(4 * j, 4 * j + 4):
                    ins = pe.transpose(ps[:, PT + j % 2, (m % 4) * 128:(m % 4 + 1) * 128], d[:, s, m::MC], ident[:])
                ins.then_inc(turned, 1)

            def build(t, s, c):
                u = 2 * t + s
                if c == 0:
                    pe.wait_ge(win_in[s], 64 * (t + 1))
                    pe.wait_ge(filt_set, 2 * (u + 1))
                if c == 1:
                    pe.wait_ge(edge_set, 4 * (u + 1))
                wait(pe, mat_set, 4 * u + c)
                r = c // 2
                stat = filt[:, s]
                if c % 2:
                    pe.matmul(ps[:, PB, 0:384], stat, edge[:, s, r], start=True, stop=True).then_inc(built, 1)
                else:
                    w = win[:, s, r]
                    src = bass.AP(w.tensor, w.offset, [list(w.ap[0]), [8, 3], [TROW, P8], [1, 16]])
                    pe.matmul(ps[:, PB, 0:384], stat, src, start=True, stop=True).then_inc(built, 1)

            def multiply(t, s, k):
                u = 2 * t + s
                if k == 0:
                    pe.wait_ge(yt_set[0], 4 * (u + 1))
                    pe.wait_ge(yt_set[1], 4 * (u + 1))
                    pe.wait_ge(mat_set, 4 * (u + 1))
                if s == 0:
                    wait(pe, gated, NB * t - 4 + k)
                else:
                    pe.wait_ge(gelu_set, NB * t + k + 1)
                if k < 4:
                    out = ps[:, PM + k, 0:IN].rearrange("p (i j b) -> p i j b", i=B, j=4)
                    nj = 4 if k < 3 else 3
                    for q in range(3):
                        ins = pe.matmul(out[:, :, 0:nj], mat[:, s, 0, 2 - q],
                                        yt[:, s, 8 * k + q:8 * k + q + 2 * nj - 1:2, :, 0:BR - 1].rearrange("p j i b -> p i j b"),
                                        start=(q == 0), stop=(q == 2))
                    if k == 3:
                        for q in range(3):
                            ins = pe.matmul(out[:, :, 3], mat[:, s, 1, 2 - q], yt[:, s, (30 + q) % MC, :, 0:BR - 1],
                                            start=(q == 0), stop=(q == 2))
                else:
                    out = ps[:, PM + 4, 0:64]
                    for q in range(3):
                        src = yt[:, s, q:q + 31:2, :, BR - 1].rearrange("p (g j) i -> p g i j", g=4)
                        ins = pe.matmul(out, mat[:, s, 2, 2 - q], src, start=(q == 0), stop=(q == 2))
                    for q in range(3):
                        ins = pe.matmul(out[:, 51:64:4], mat[:, s, 3, 2 - q], yt[:, s, (30 + q) % MC, :, BR - 1],
                                        start=(q == 0), stop=(q == 2))
                ins.then_inc(prod, 1)

            def prepare_step(t, s, k):
                turn(t, s, 2 * k)
                turn(t, s, 2 * k + 1)
                build(t, s, k)

            def run(t, s, tn, sn):
                for k in range(4):
                    multiply(t, s, k)
                    if tn is not None:
                        prepare_step(tn, sn, k)
                multiply(t, s, 4)
            pe.wait_ge(clear, 1)
            tasks(pe, lambda: [prepare_step(0, 0, k) for k in range(4)], run)

        def copy_turned(eng, copy, t, s, j):
            u = 2 * t + s
            eng.wait_ge(turned, 8 * u + j + 1)
            copy(yt[:, s, 4 * j:4 * j + 4].rearrange("p a b c -> p (a b c)"), ps[:, PT + j % 2, :]).then_inc(yt_set[j % 2], 1)

        @block.scalar
        def _(act):
            def filters(t, s):
                act.wait_ge(win_in[s], 64 * (t + 1))
                for r in range(2):
                    half = slice(64 * r, 64 * r + 64)
                    w = fwin[half, s]
                    src = bass.AP(w.tensor, w.offset, [list(w.ap[0]), [16, 8], [1, 8]])
                    act.copy(filt[half, s, half].rearrange("p (a b) -> p a b", a=8), src).then_inc(filt_set, 1)

            def prepare_step(t, s, k):
                u = 2 * t + s
                if k == 0:
                    filters(t, s)
                copy_turned(act, act.copy, t, s, 2 * k)
                act.wait_ge(built, 4 * u + k + 1)
                act.copy(mat[:, s, k].rearrange("p a b -> p (a b)"), ps[:, PB, 0:384]).then_inc(mat_set, 1)

            def run(t, s, tn, sn):
                u = 2 * t + s
                for k in range(NB):
                    if s == 0:
                        act.wait_ge(prod, NB * u + k + 1)
                        wait(act, gated, NB * t - 4 + k)
                        if k < 4:
                            act.activation(g1[:, k], ps[:, PM + k, 0:IN], AF.Gelu).then_inc(gelu_set, 1)
                        else:
                            act.activation(g1w[:], ps[:, PM + 4, 0:64], AF.Gelu).then_inc(gelu_set, 1)
                    if k < 4 and tn is not None:
                        prepare_step(tn, sn, k)
            act.wait_ge(clear, 1)
            tasks(act, lambda: [prepare_step(0, 0, k) for k in range(4)], run)

        @block.vector
        def _(v):
            v.memset(filt[:], 0.0)
            v.memset(win[:], 0.0)
            v.memset(zero[:], 0.0)
            v.memset(yt[:, :, MC], 0.0).then_inc(clear, 1)

            def edges(t, s):
                u = 2 * t + s
                v.wait_ge(win_in[s], 64 * (t + 1))
                for r in range(2):
                    w = win[:, s, r]
                    src = bass.AP(w.tensor, w.offset, [list(w.ap[0]), [8, 3], [TROW, P8], [1, 16]])
                    v.tensor_tensor(edge[:, s, r], src, keep["mask"][:].rearrange("p (a b c) -> p a b c", a=3, b=P8), ALU.mult
                                    ).then_inc(edge_mul, 1)
                v.wait_ge(edge_mul, 2 * (u + 1))
                for r in range(2):
                    for q in range(2):
                        dst = edge[:, s, r, 1 - q, :, 11 + 2 * q:13 + 2 * q]
                        v.scalar_tensor_tensor(dst, xwin[:, s, r, :, 2 * q:2 * q + 2], keep["xmask"][:, q:q + 1], dst,
                                               ALU.mult, ALU.add).then_inc(edge_set, 1)

            def prepare_step(t, s, k):
                if k == 0:
                    edges(t, s)
                copy_turned(v, v.tensor_copy, t, s, 2 * k + 1)

            def run(t, s, tn, sn):
                u = 2 * t + s
                for k in range(NB):
                    if s == 1:
                        v.wait_ge(prod, NB * u + k + 1)
                        v.wait_ge(clipped, NB * t + k + 1)
                        if k == 0:
                            wait(v, g_out, 16 * t)
                        if k < 4:
                            v.scalar_tensor_tensor(gt[:, k, :, 0:BR - 1], ps[:, PM + k, 0:IN].rearrange("p (a b) -> p a b", a=16), 0.0,
                                                   g1[:, k].rearrange("p (a b) -> p a b", a=16), ALU.max, ALU.mult).then_inc(gated, 1)
                        else:
                            v.scalar_tensor_tensor(gt[:, :, :, BR - 1].rearrange("p a b -> p (a b)"), ps[:, PM + 4, 0:64], 0.0, g1w[:],
                                                   ALU.max, ALU.mult).then_inc(gated, 1)
                    if k < 4 and tn is not None:
                        prepare_step(tn, sn, k)
            tasks(v, lambda: [prepare_step(0, 0, k) for k in range(4)], run)

        @block.gpsimd
        def _(pool):
            def run(t, s, tn, sn):
                if s == 0:
                    for k in range(NB):
                        pool.wait_ge(gelu_set, NB * t + k + 1)
                        part = g1[:, k] if k < 4 else g1w[:]
                        pool.tensor_tensor(held[:, k:k + 1], zero[:], zero[:], ALU.add)
                        pool.tensor_scalar(part, part, 0.0, None, ALU.max).then_inc(clipped, 1)
                else:
                    pool.wait_ge(gated, NB * (t + 1))
                    pool.dma_start(dram(scratch["g"], t * (128 * TILES), [[TILES, 128], [1, TILES]]),
                                   gt[:].rearrange("p a b c -> p (a b c)")).then_inc(g_out, 16)
            pool.wait_ge(clear, 1)
            tasks(pool, lambda: None, run)
            pool.wait_ge(g_out, 16 * HID)


def stage_d(nc, io, keep, scratch):
    NP = 16 * 512
    with ExitStack() as ctx:
        sb = lambda name, shape: ctx.enter_context(nc.sbuf_tensor(name, shape, F32))
        sem = lambda name: ctx.enter_context(nc.semaphore(name))
        ps = ctx.enter_context(nc.psum_tensor("psD", [128, 8, 512], F32))
        g = sb("g", [DIM, 2, 2, NP])
        xt = sb("xt", [DIM, 2, BR, W])
        g_in = [sem(f"gd_in{k}") for k in range(2)]
        x_in = [sem(f"xd_in{k}") for k in range(2)]
        mm = sem("mm_d")
        added = sem("added")
        out_st = [sem(f"out_st{k}") for k in range(2)]
        block = ctx.enter_context(nc.Block())
        moves = lambda p: 16 if p < 5 else 32
        before = lambda p: sum(moves(q) for q in range(p % 2, p, 2))
        total = [before(8 + k) for k in range(2)]

        def rows(ap, img, p, slot):
            top = OFF + p
            full = BR if top < 8 else BR - 1
            yield dram(ap, img * (DIM * PIX) + top * W, [[PIX, DIM], [ROWPIX, full], [1, W]]), xt[:, slot, 0:full]
            if full < BR:
                yield dram(ap, img * (DIM * PIX) + (top - 8) * W, [[PIX, DIM], [1, W]]), xt[:, slot, BR - 1]

        def each(eng, strip):
            over(eng, B, lambda img: [strip(img, p, 8 * img + p, p % 2) for p in range(P8)])

        @block.sync
        def _(sp):
            def load(img, p, n, slot):
                wait(sp, mm, 16 * (n - 1))
                for kt in range(2):
                    sp.dma_start(g[:, slot, kt].rearrange("p (a b) -> p a b", b=128),
                                 dram(scratch["g"], kt * DIM * 128 * TILES + p * 16 * TILES + img * 128,
                                      [[128 * TILES, DIM], [512, 64], [1, 128]])).then_inc(g_in[slot], 16)
                wait(sp, out_st[slot], img * total[slot] + before(p))
                for far, near in rows(io["x"], img, p, slot):
                    sp.dma_start(near, far).then_inc(x_in[slot], 16)
            each(sp, load)

        @block.tensor
        def _(pe):
            def strip(img, p, n, slot):
                pe.wait_ge(g_in[slot], 32 * 4 * img + 32 * (p // 2 + 1))
                for c in range(16):
                    wait(pe, added, 16 * n + c - 7)
                    for kt in range(2):
                        ins = pe.matmul(ps[0:DIM, c % 8, :], keep["w_outT"][:, kt], g[:, slot, kt, c * 512:(c + 1) * 512],
                                        start=(kt == 0), stop=(kt == 1))
                    ins.then_inc(mm, 1)
            each(pe, strip)

        @block.vector
        def _(v):
            def strip(img, p, n, slot):
                v.wait_ge(x_in[slot], img * total[slot] + before(p) + moves(p))
                for c in range(16):
                    v.wait_ge(mm, 16 * n + c + 1)
                    nj = TJ if c < 13 else TJ - 1
                    if nj < TJ:
                        dst = xt[:, slot, :, c - 13]
                        v.tensor_tensor(dst, ps[0:DIM, c % 8, nj * BR:], dst, ALU.add)
                    dst = xt[:, slot, :, OFF + c:OFF + c + 16 * (nj - 1) + 1:16].rearrange("p b j -> p j b")
                    v.tensor_tensor(dst, ps[0:DIM, c % 8, 0:nj * BR].rearrange("p (j b) -> p j b", b=BR), dst, ALU.add).then_inc(added, 1)
            each(v, strip)

        @block.scalar
        def _(act):
            def store(img, p, n, slot):
                act.wait_ge(added, 16 * (n + 1))
                for far, near in rows(io["out"], img, p, slot):
                    act.dma_start(far, near).then_inc(out_st[slot], 16)
            each(act, store)
            for k in range(2):
                act.wait_ge(out_st[k], B * total[k])


def build(nc, io):
    with ExitStack() as ctx:
        sb = lambda name, shape: ctx.enter_context(nc.sbuf_tensor(name, shape, F32))
        keep = {
            "ident": sb("ident", [128, 128]),
            "mask": sb("mask", [128, 384]),
            "xmask": sb("xmask", [128, 2]),
            "w_inT": sb("w_inT", [DIM, C2]),
            "w_outT": sb("w_outT", [DIM, 2, DIM]),
            "scale": sb("scale", [DIM, B]),
            "shift": sb("shift", [DIM, B]),
        }
        scratch = {
            "kper": nc.dram_tensor("kper_d", [C2, KTAB], F32).ap(),
            "tab": nc.dram_tensor("tab_d", [C2, TAB], F32).ap(),
            "xtab": nc.dram_tensor("xtab_d", [C2, XTAB], F32).ap(),
            "y": [nc.dram_tensor(f"y{s}_d", [HID, B * (BR + 1) * ROWPIX], F32).ap() for s in range(2)],
            "g": nc.dram_tensor("g_d", [HID, 128 * TILES], F32).ap(),
        }
        stage_a(nc, io, keep, scratch)
        stage_b(nc, io, keep, scratch)
        stage_c(nc, keep, scratch)
        stage_d(nc, io, keep, scratch)


def constants():
    import numpy as np
    ident = np.eye(128, dtype=np.float32)
    group = np.zeros((DIM, DIM), np.float32)
    for k in range(DIM):
        group[k, k // 3 * 3:k // 3 * 3 + 3] = 1.0 / 3
    u, v = np.meshgrid(np.arange(8), np.arange(5), indexing="ij")
    weight = np.where((v == 0) | (v == 4), 1.0, 2.0) / 64
    i, j = np.meshgrid(np.arange(15), np.arange(16), indexing="ij")
    dft = weight.reshape(40, 1) * np.cos(2 * np.pi * (u.reshape(40, 1) * (i.reshape(1, -1) - 7) + v.reshape(40, 1) * (j.reshape(1, -1) - 7)) / 8)
    col = 7 - np.arange(128) % 8
    mask = np.zeros((128, 3, 8, 16), np.float32)
    for q in range(3):
        for c in range(16):
            mask[:, q, :, c] = ((8 * (2 - q) + col < 16) == (OFF + c < 16))[:, None]
    xmask = -np.stack([col == 7, col == 0], 1).astype(np.float32)
    return {"ident": ident, "group": group, "dft": dft.astype(np.float32), "mask": mask.reshape(128, 384), "xmask": xmask}


_INS = {"x": "x", "w_in": "L0_conv_w_in", "w_dw": "L0_conv_w_dw", "w_dw3": "L0_conv_w_dw3", "w_dw5": "L0_conv_w_dw5",
        "filt": "L0_conv_fft_filt", "w_out": "L0_conv_w_out"}


def kernel(**inputs):
    import numpy as _np
    import concourse.bacc as _bacc
    from concourse import mybir as _mybir
    from concourse.bass_utils import run_bass_kernel_spmd as _run

    nc = _bacc.Bacc("TRN2", target_bir_lowering=False, num_devices=1)
    arrays, io = {}, {}
    for name, full in _INS.items():
        arrays[f"in_{name}"] = _np.ascontiguousarray(inputs[full])
    for name, value in constants().items():
        arrays[f"in_{name}"] = value
    for name, a in arrays.items():
        io[name[3:]] = nc.dram_tensor(name, a.shape, _mybir.dt.from_np(a.dtype), kind="ExternalInput").ap()
    io["out"] = nc.dram_tensor("out_0", (B, DIM, H, W), _mybir.dt.float32, kind="ExternalOutput").ap()
    build(nc, io)
    r = _run(nc, [arrays], core_ids=[0])
    return r.results[0]["out_0"]
```

```python
from contextlib import ExitStack

import concourse.bass as bass
from concourse import mybir

F32 = mybir.dt.float32
F32R = mybir.dt.float32r
ALU = mybir.AluOpType
AF = mybir.ActivationFunctionType

B, DIM, H, W = 4, 96, 256, 256
HID = 2 * DIM
C2 = 2 * HID
PIX = H * W
P8 = 8
BR = H // P8
MC = W // P8
TJ = W // 16
OFF = 3
ROWPIX = P8 * W
CT = C2 // 128
NIDX = 14
TROW = NIDX + 8
ZT = 16
TAB = ZT * 2 * P8 * TROW
WIN = (2 * P8 - 1) * TROW + NIDX
XTAB = ZT * 2 * P8 * 4
KTAB = 15 * 16
KWIN = 7 * 16 + 8
NE = 11
NCOL = NIDX + 4
TILES = B * BR * TJ
TILES2 = B * BR * MC
EPS = 1e-5
EDGE = [(0, 4), (0, 3), (2, 1), (2, 0)]


def wait(eng, sem, value):
    if not isinstance(value, int) or value > 0:
        eng.wait_ge(sem, value)


def over(eng, n, body):
    body(0)
    with eng.Fori(1, n) as i:
        body(i)


def dram(tensor, offset, dims):
    return bass.AP(tensor.tensor, offset, dims)


def stage_a(nc, io, keep, scratch):
    CH = 2048
    NCH = PIX // CH
    RING = 4
    with ExitStack() as ctx:
        sb = lambda name, shape: ctx.enter_context(nc.sbuf_tensor(name, shape, F32))
        sem = lambda name: ctx.enter_context(nc.semaphore(name))
        ps = ctx.enter_context(nc.psum_tensor("psA", [128, 8, 512], F32))
        xs = sb("xsA", [DIM, RING, CH])
        stats = sb("stats", [DIM, NCH * CH // 512, 6])
        mv = sb("mv", [DIM, B, 2])
        small = sb("small", [DIM, 10, B])
        win = sb("win", [128, CT, DIM])
        wout = sb("wout", [DIM, HID])
        filt = sb("filt", [128, CT, 40])
        filtT = sb("filtT", [40, C2])
        dft = sb("dft", [40, KTAB])
        group = sb("group", [DIM, DIM])
        kper = sb("kper", [128, CT, KTAB])
        w1 = sb("w1", [128, CT, 9])
        w2 = sb("w2", [128, CT, 25])
        prod = sb("prod", [128, CT, 3, 5])
        h = sb("h", [128, NE, CT, 3, 5])
        cf = sb("cf", [128, CT, 7, NE])
        tab = sb("tab", [128, CT, ZT, 2, P8, TROW])
        xtab = sb("xtab", [128, CT, ZT, 2, P8, 4])
        x_in = [sem(f"x_in{k}") for k in range(RING)]
        x_used = sem("x_used")
        params = sem("params")
        w2_clear = sem("w2_clear")
        w2_in = sem("w2_in")
        turned = sem("turned")
        turned_sb = sem("turned_sb")
        kper_ps = sem("kper_ps")
        kper_sb = sem("kper_sb")
        aggr = sem("aggr")
        seg = sem("seg")
        g_mean = sem("g_mean")
        g_in = sem("g_in")
        g_var = sem("g_var")
        var_eps = sem("var_eps")
        root = sem("root")
        vchain = sem("vchain")
        pchain = sem("pchain")
        tab_ready = sem("tab_ready")
        tab_out = sem("tab_out")
        kper_out = sem("kper_out")
        block = ctx.enter_context(nc.Block())

        @block.sync
        def _(sp):
            for dst, src in ((keep["ident"][:], io["ident"]), (keep["xmask"][:], io["xmask"]),
                             (dft[:], io["dft"]), (group[:], io["group"]), (wout[:], io["w_out"]),
                             (win[:], io["w_in"].rearrange("(t p) c -> p t c", p=128)),
                             (filt[:], io["filt"].rearrange("(t p) a b u v -> p t (a b u v)", p=128)),
                             (w1[:], io["w_dw"].rearrange("(t p) a u v -> p t (a u v)", p=128))):
                sp.dma_start(dst, src).then_inc(params, 16)
            sp.wait_ge(w2_clear, 1)
            w3 = io["w_dw3"].rearrange("o a u v -> o (a u) v")
            w5 = io["w_dw5"].rearrange("o a u v -> o (a u v)")
            mid = w2[:].rearrange("p t (u v) -> p t u v", u=5)[:, :, 1:4, 1:4]
            sp.dma_start(mid[:, 0], w3[0:128]).then_inc(w2_in, 16)
            sp.dma_start(mid[0:64, 1], w3[128:192]).then_inc(w2_in, 16)
            sp.dma_start(w2[64:128, 1], w5[0:64]).then_inc(w2_in, 16)
            sp.dma_start(w2[:, 2], w5[64:192]).then_inc(w2_in, 16)

            def load(img, q):
                for k in range(RING):
                    n = img * (NCH) + q * RING + k
                    wait(sp, x_used, n - (RING - 1))
                    sp.dma_start(xs[:, k], dram(io["x"], img * (DIM * PIX) + (q * RING + k) * CH, [[PIX, DIM], [1, CH]])
                                 ).then_inc(x_in[k], 16)
            for img in range(B):
                over(sp, NCH // RING, lambda q, img=img: load(img, q))

        @block.vector
        def _(v):
            def chain(ins):
                chain.n += 1
                ins.then_inc(vchain, 1)
                v.wait_ge(vchain, chain.n)
            chain.n = 0
            v.memset(w2[:], 0.0).then_inc(w2_clear, 1)

            def chunk_stats(img, q):
                for k in range(RING):
                    v.wait_ge(x_in[k], (img * (NCH // RING) + q + 1) * 16)
                    for j in range(CH // 512):
                        at = (q * RING + k) * (CH // 512) + j
                        ins = v.bn_stats(stats[:, at, :] if isinstance(at, int) else stats[:, bass.ds(at, 1), :],
                                         xs[:, k, j * 512:(j + 1) * 512])
                    ins.then_inc(x_used, 1)
            for img in range(B):
                if img:
                    v.wait_ge(aggr, img)
                over(v, NCH // RING, lambda q, img=img: chunk_stats(img, q))
                v.wait_ge(x_used, NCH * (img + 1))
                v.bn_aggr(mv[:, img, :], stats[:].rearrange("p a b -> p (a b)")).then_inc(aggr, 1)
            mg, dev, dv2, vin, ve, sd, r, t1, t2, t3 = (small[:, k, :] for k in range(10))
            v.wait_ge(g_mean, 1)
            chain(v.tensor_copy(mg, ps[0:DIM, 5, 0:B]))
            chain(v.tensor_tensor(dev, mv[:, :, 0], mg, ALU.subtract))
            chain(v.tensor_tensor(dv2, dev, dev, ALU.mult))
            v.tensor_tensor(vin, dv2, mv[:, :, 1], ALU.add).then_inc(g_in, 1)
            v.wait_ge(g_var, 1)
            v.tensor_scalar(ve, ps[0:DIM, 6, 0:B], EPS, None, ALU.add).then_inc(var_eps, 1)
            v.wait_ge(root, 1)
            chain(v.reciprocal(r, sd))
            v.wait_ge(var_eps, 1)
            chain(v.tensor_tensor(t1, r, r, ALU.mult))
            chain(v.tensor_tensor(t2, t1, ve, ALU.mult))
            chain(v.tensor_scalar(t3, t2, -0.5, 1.5, ALU.mult, ALU.add))
            chain(v.tensor_tensor(keep["scale"][:], r, t3, ALU.mult))
            chain(v.tensor_tensor(dev, mg, keep["scale"][:], ALU.mult))
            v.tensor_scalar(keep["shift"][:], dev, -1.0, None, ALU.mult)

        @block.tensor
        def _(pe):
            pe.wait_ge(params, 16 * 8)
            ident = keep["ident"]
            for t in range(CT):
                pe.transpose(ps[0:DIM, 0, t * 128:(t + 1) * 128], win[:, t, :], ident[:])
            for t in range(CT):
                pe.transpose(ps[0:40, 1, t * 128:(t + 1) * 128], filt[:, t, :], ident[:])
            for t in range(2):
                ins = pe.transpose(ps[0:DIM, 2, t * DIM:(t + 1) * DIM], wout[:, t * DIM:(t + 1) * DIM], ident[0:DIM, 0:DIM])
            ins.then_inc(turned, 1)
            pe.wait_ge(turned_sb, 1)
            for t in range(CT):
                ins = pe.matmul(ps[:, 3 + t // 2, (t % 2) * KTAB:(t % 2 + 1) * KTAB], filtT[:, t * 128:(t + 1) * 128], dft[:],
                                start=True, stop=True)
            ins.then_inc(kper_ps, 1)
            pe.wait_ge(aggr, B)
            pe.matmul(ps[0:DIM, 5, 0:B], group[:], mv[:, :, 0], start=True, stop=True).then_inc(g_mean, 1)
            pe.wait_ge(g_in, 1)
            pe.matmul(ps[0:DIM, 6, 0:B], group[:], small[:, 3, :], start=True, stop=True).then_inc(g_var, 1)

        @block.scalar
        def _(act):
            act.wait_ge(turned, 1)
            act.copy(filtT[:], ps[0:40, 1, 0:C2]).then_inc(turned_sb, 1)
            act.copy(keep["w_inT"][:], ps[0:DIM, 0, 0:C2])
            act.copy(keep["w_outT"][:].rearrange("p a b -> p (a b)"), ps[0:DIM, 2, 0:2 * DIM])
            act.wait_ge(kper_ps, 1)
            act.copy(kper[:, 0:2].rearrange("p a b -> p (a b)"), ps[:, 3, 0:2 * KTAB]).then_inc(kper_sb, 1)
            act.copy(kper[:, 2], ps[:, 4, 0:KTAB]).then_inc(kper_sb, 1)
            act.wait_ge(kper_sb, 2)
            act.dma_start(scratch["kper"].rearrange("(t p) k -> p t k", p=128), kper[:]).then_inc(kper_out, 16)
            act.wait_ge(tab_ready, 1)
            for t in range(CT):
                act.dma_start(scratch["tab"][t * 128:(t + 1) * 128], tab[:, t].rearrange("p a b c d -> p (a b c d)")).then_inc(tab_out, 16)
                act.dma_start(scratch["xtab"][t * 128:(t + 1) * 128], xtab[:, t].rearrange("p a b c d -> p (a b c d)")).then_inc(tab_out, 16)
            act.wait_ge(var_eps, 1)
            act.activation(small[:, 5, :], small[:, 4, :], AF.Sqrt).then_inc(root, 1)
            act.wait_ge(kper_out, 16)
            act.wait_ge(tab_out, 32 * CT)

        @block.gpsimd
        def _(pool):
            def chain(ins):
                chain.n += 1
                ins.then_inc(pchain, 1)
                pool.wait_ge(pchain, chain.n)
            chain.n = 0
            pool.memset(tab[:], 0.0)
            pool.memset(xtab[:], 0.0)
            chain(pool.memset(h[:], 0.0))
            pool.wait_ge(params, 16 * 8)
            pool.wait_ge(w2_in, 64)
            w1v = w1[:].rearrange("p t (a b) -> p t a b", a=3)
            w2v = w2[:].rearrange("p t (a b) -> p t a b", a=5)

            def rows_outer(ac, bc):
                chain(pool.tensor_tensor(prod[:], w1v[:, :, :, ac:ac + 1].broadcast_to([128, CT, 3, 5]),
                                         w2v[:, :, :, bc].unsqueeze(2).broadcast_to([128, CT, 3, 5]), ALU.mult))
            for ac in range(3):
                for bc in range(5):
                    rows_outer(ac, bc)
                    e = 6 - ac - bc
                    chain(pool.tensor_tensor(h[:, e], h[:, e], prod[:], ALU.add))
            for k, (ac, bc) in enumerate(EDGE):
                rows_outer(ac, bc)
                chain(pool.tensor_copy(h[:, 7 + k], prod[:]))
            chain(pool.memset(cf[:], 0.0))
            for a in range(3):
                for t in range(CT):
                    dst = cf[:, t, a:a + 5, :]
                    ins = pool.tensor_tensor(dst, dst, h[:, :, t, a, :].rearrange("p e b -> p b e"), ALU.add)
                chain(ins) if a == 2 else chain(ins)
            for z in range(ZT):
                zt = 7 - z if z < 8 else 23 - z
                for p in range(P8):
                    d = z - p
                    if not 0 <= d <= 6:
                        continue
                    for r in range(2):
                        if r == 1 and (z < 8) != (p + OFF < 8):
                            continue
                        pool.tensor_copy(tab[:, :, zt, r, p, 7:14], cf[:, :, d, 0:7])
                        ins = pool.tensor_copy(xtab[:, :, zt, r, p, :], cf[:, :, d, 7:NE])
            chain(ins)
            for z, p, a, b in ((7, 3, 0, 4), (7, 4, 0, 3), (8, 5, 2, 1), (8, 6, 2, 0)):
                zt = 7 - z if z < 8 else 23 - z
                for dst, e0, e1 in ((tab[:, :, zt, 1, p, 7:14], 0, 7), (xtab[:, :, zt, 1, p, :], 7, NE)):
                    ins = pool.tensor_tensor(dst, dst, h[:, e0:e1, :, a, b].rearrange("p e t -> p t e"), ALU.subtract)
            ins.then_inc(tab_ready, 1)


def stage_b(nc, io, keep, scratch):
    G = 4
    NG = BR // G
    NS = CT * G * 2
    by = lambda n: n % 3 == 2
    before = lambda n: sum(by(k) == by(n) for k in range(n))
    with ExitStack() as ctx:
        sb = lambda name, shape: ctx.enter_context(nc.sbuf_tensor(name, shape, F32))
        sem = lambda name: ctx.enter_context(nc.semaphore(name))
        ps = ctx.enter_context(nc.psum_tensor("psB", [128, 4, 1024], F32))
        xs = sb("xsB", [DIM, G, ROWPIX])
        xn = sb("xn", [DIM, 2, G, ROWPIX])
        y = sb("y", [128, CT, P8 * P8, G, MC])
        x_in = [sem(f"xb_in{k}") for k in range(G)]
        scaled = sem("scaled")
        normed = sem("normed")
        mm = sem("mm")
        copied = {False: sem("by_dve"), True: sem("by_act")}
        each_group = {e: sum(by(n) == e for n in range(NS)) for e in (False, True)}
        stored = [sem(f"y_stored{t}") for t in range(CT)]
        parts = ((0, 0, 128, 0, 0), (1, 0, 64, 0, 128), (1, 64, 128, 1, 0), (2, 0, 128, 1, 64))
        nparts = [sum(p[0] == t for p in parts) for t in range(CT)]
        CHS = B * PIX
        block = ctx.enter_context(nc.Block())

        def groups(eng, group):
            for img in range(B):
                over(eng, NG // 2, lambda i, img=img: [group(img, 2 * i + par, NG * img + 2 * i + par, par) for par in range(2)])

        @block.sync
        def _(sp):
            def load(img, q, g, par):
                for k in range(G):
                    wait(sp, normed, G * g + k - (G - 1))
                    sp.dma_start(xs[:, k], dram(io["x"], img * (DIM * PIX) + (q * G + k) * ROWPIX, [[PIX, DIM], [1, ROWPIX]])
                                 ).then_inc(x_in[k], 16)
            groups(sp, load)

        @block.gpsimd
        def _(pool):
            def norm(img, q, g, par):
                for k in range(G):
                    pool.wait_ge(x_in[k], g * 16 + 16)
                    if k == 0:
                        wait(pool, mm, NS * (g - 1))
                    pool.tensor_tensor(xn[:, par, k], xs[:, k], keep["scale"][:, img:img + 1].broadcast_to([DIM, ROWPIX]), ALU.mult
                                       ).then_inc(scaled, 1)
                    pool.wait_ge(scaled, G * g + k + 1)
                    pool.tensor_tensor(xn[:, par, k], xn[:, par, k], keep["shift"][:, img:img + 1].broadcast_to([DIM, ROWPIX]), ALU.add
                                       ).then_inc(normed, 1)
            groups(pool, norm)

        @block.tensor
        def _(pe):
            def group(img, q, g, par):
                for n in range(NS):
                    t, k, half = n // (2 * G), n // 2 % G, n % 2
                    if t == 0 and half == 0:
                        pe.wait_ge(normed, G * g + k + 1)
                    old, og = (n - 4, g) if n >= 4 else (n + NS - 4, g - 1)
                    if not (isinstance(og, int) and og < 0):
                        pe.wait_ge(copied[by(old)], each_group[by(old)] * og + before(old) + 1)
                    for c in range(2):
                        at = half * 1024 + c * 512
                        ins = pe.matmul(ps[:, n % 4, c * 512:(c + 1) * 512], keep["w_inT"][:, t * 128:(t + 1) * 128],
                                        xn[:, par, k, at:at + 512], start=True, stop=True)
                    ins.then_inc(mm, 1)
            groups(pe, group)

        def copy_out(eng, copy, me, img, q, g, par, ts):
            for n in range(NS):
                t, k, half = n // (2 * G), n // 2 % G, n % 2
                if by(n) != me or t not in ts:
                    continue
                if before(n) == 0 or n - 3 < t * 2 * G:
                    wait(eng, stored[t], 16 * nparts[t] * g)
                eng.wait_ge(mm, NS * g + n + 1)
                copy(y[:, t, 32 * half:32 * half + 32, k].rearrange("p (r c) m -> p r c m", r=4),
                     ps[:, n % 4].rearrange("p (r m c) -> p r c m", r=4, c=8)).then_inc(copied[me], 1)

        @block.vector
        def _(v):
            groups(v, lambda *a: copy_out(v, v.tensor_copy, False, *a, range(CT)))

        @block.scalar
        def _(act):
            def group(img, q, g, par):
                for t in range(CT):
                    copy_out(act, act.copy, True, img, q, g, par, (t,))
                    for e in (False, True):
                        last = max(n for n in range(2 * G * (t + 1)) if by(n) == e)
                        act.wait_ge(copied[e], each_group[e] * g + before(last) + 1)
                    for pt, p0, p1, half, c0 in parts:
                        if pt == t:
                            act.dma_start(dram(scratch["y"][half], c0 * CHS + img * (BR * MC) + q * (G * MC),
                                               [[CHS, p1 - p0], [TILES2, P8 * P8], [1, G * MC]]),
                                          y[p0:p1, t].rearrange("p a b c -> p a (b c)")).then_inc(stored[t], 16)
            groups(act, group)
            for t in range(CT):
                act.wait_ge(stored[t], 16 * nparts[t] * B * NG)


def stage_c(nc, keep, scratch):
    NB = 5
    NR = 2 * P8
    WIDE = (0, 1, 3)
    EDGED = (0, 2, 4)
    PASSES = ((0, 0), (1, 0), (0, 1))
    QUART = TILES2 // 4
    with ExitStack() as ctx:
        sb = lambda name, shape, dt=F32: ctx.enter_context(nc.sbuf_tensor(name, shape, dt))
        sem = lambda name: ctx.enter_context(nc.semaphore(name))
        ps = ctx.enter_context(nc.psum_tensor("psC", [128, 8, 512], F32))
        PB, PM = 0, 1
        d = sb("d", [128, 2, B, BR, MC])
        yt = [sb(f"yt{k}", [128, 2, TILES2], F32R) for k in range(2)]
        ywrap = sb("ywrap", [128, 2, B * MC + 2])
        yedge = sb("yedge", [128, 2, 3, B * BR])
        win = sb("win_c", [128, 2, NR, TROW])
        xwin = sb("xwin", [128, 2, NR, 4])
        fwin = sb("fwin", [128, 2, KWIN])
        filt = sb("filt_c", [128, 2, 128])
        edge = sb("edge", [128, 2, NR, 4])
        cols = sb("cols", [128, 2, NR, NCOL])
        cols2 = sb("cols2", [128, 2, 2, P8, NIDX], F32R)
        mat = sb("mat", [128, 2, 2, 5, P8, 16])
        mat2 = sb("mat2", [128, 2, 2, 3, P8, 16], F32R)
        g1 = sb("g1", [128, 4, 512])
        g1w = sb("g1w", [128, 64])
        gt = sb("gt", [128, B, BR, TJ])
        zero = sb("zero", [128, 1])
        held = sb("held", [128, 2])
        d_in = [sem(f"d_in{s}") for s in range(2)]
        win_in = [sem(f"win_in{s}") for s in range(2)]
        clear = sem("clear")
        high_set = sem("high_set")
        low_set = sem("low_set")
        wrap_set = sem("wrap_set")
        yedge_set = sem("yedge_set")
        edge_set = sem("edge_set")
        filt_set = sem("filt_set")
        built = sem("built")
        cols_set = sem("cols_set")
        cols_high = sem("cols_high")
        cols_low = sem("cols_low")
        mat_set = sem("mat_set")
        prod = sem("prod_c")
        gelu_set = sem("gelu_set")
        gated = sem("gated")
        g_out = sem("g_out")
        CHS = B * PIX
        CLEARS = 7
        block = ctx.enter_context(nc.Block())

        def tasks(eng, prepare, run):
            def pair(t, last=False):
                run(t, 0, (t, 1), None if last else (t + 1, 0))
                run(t, 1, None if last else (t + 1, 0), None if last else (t + 1, 1))
            prepare(0, 0)
            pair(0)
            with eng.Fori(1, HID - 1) as t:
                pair(t)
            pair(HID - 1, True)

        @block.sync
        def _(sp):
            sp.wait_ge(clear, CLEARS)

            def load(t, s):
                u = 2 * t + s
                ys = scratch["y"][s]
                wait(sp, built, u - 1)
                c = t + s * HID
                sp.dma_start(win[:, s].rearrange("p a b -> p (a b)")[:, 0:WIN],
                             dram(scratch["tab"], c * TAB, [[NR * TROW, ZT], [1, 8], [1, WIN]])).then_inc(win_in[s], 16)
                sp.dma_start(xwin[:, s].rearrange("p a b -> p (a b)"),
                             dram(scratch["xtab"], c * XTAB, [[64, ZT], [0, 8], [1, 64]])).then_inc(win_in[s], 16)
                for r in range(2):
                    sp.dma_start(fwin[64 * r:64 * r + 64, s],
                                 dram(scratch["kper"], c * KTAB, [[16, 8], [1, 8], [1, KWIN]])).then_inc(win_in[s], 16)
                wait(sp, low_set, 4 * (u - 1))
                sp.dma_start(d[0:64, s].rearrange("p i b m -> p (i b m)"), dram(ys, t * CHS, [[TILES2, 64], [1, TILES2]])).then_inc(d_in[s], 16)
                sp.dma_start(d[64:128, s, :, 0:BR - 1].rearrange("p i b m -> p i (b m)"),
                             dram(ys, t * CHS + MC, [[TILES2, 64], [BR * MC, B], [1, (BR - 1) * MC]])).then_inc(d_in[s], 16)

            def store(t):
                sp.wait_ge(gated, NB * (t + 1))
                sp.dma_start(dram(scratch["g"], t * (128 * TILES), [[TILES, 128], [1, TILES]]),
                             gt[:].rearrange("p a b c -> p (a b c)")).then_inc(g_out, 16)

            for t in range(2):
                load(t, 0)
                load(t, 1)
            with sp.Fori(2, HID) as t:
                load(t, 0)
                store(t - 2)
                load(t, 1)
            store(HID - 2)
            store(HID - 1)
            sp.wait_ge(g_out, 16 * HID)

        @block.tensor
        def _(pe):
            def build(t, s):
                u = 2 * t + s
                pe.wait_ge(filt_set, 2 * (u + 1))
                pe.wait_ge(edge_set, 2 * (u + 1))
                wait(pe, cols_set, u)
                out = ps[:, PB, 0:NR * NCOL].rearrange("p (a b) -> p a b", b=NCOL)
                pe.matmul(out[:, :, 0:NIDX], filt[:, s], win[:, s, :, 0:NIDX], start=True, stop=True)
                pe.matmul(out[:, :, NIDX:NCOL], filt[:, s], edge[:, s], start=True, stop=True).then_inc(built, 1)

            def wide(out, s, src):
                for n in range(9):
                    q, (pm, py) = n // 3, PASSES[n % 3]
                    ins = pe.matmul(out, mat2[:, s, pm, q].rearrange("p a b -> p (a b)"), src(yt[py][:, s], q), start=(n == 0), stop=(n == 8))
                return ins

            def narrow(out, s, row, kinds, src):
                for q in range(3):
                    ins = pe.matmul(out, mat[:, s, row, kinds[q]].rearrange("p a b -> p (a b)"), src(q), start=(q == 0), stop=(q == 2))
                return ins

            def multiply(t, s, k):
                u = 2 * t + s
                if k == 0:
                    pe.wait_ge(low_set, 4 * (u + 1))
                    pe.wait_ge(wrap_set, 2 * (u + 1))
                    pe.wait_ge(yedge_set, 2 * (u + 1))
                    pe.wait_ge(mat_set, u + 1)
                if s == 0:
                    wait(pe, gated, NB * t - 4 + k)
                else:
                    pe.wait_ge(gelu_set, NB * t + k + 1)
                if k < 3:
                    ins = wide(ps[:, PM + k].rearrange("p (n j) -> p n j", j=4), s, lambda y, q:
                               y.rearrange("p (n m) -> p n m", m=MC)[:, :, 8 * k + q:8 * k + q + 7:2])
                elif k == 3:
                    wide(ps[:, PM + 3, 0:384].rearrange("p (j n) -> p j n", j=3), s, lambda y, q:
                         y.rearrange("p (n m) -> p m n", m=MC)[:, 24 + q:24 + q + 5:2])
                    ins = narrow(ps[:, PM + 3, 384:512], s, 0, EDGED, lambda q: yedge[:, s, q])
                else:
                    out = ps[:, PM + 4, 0:64].rearrange("p (i j) -> p i j", i=B)
                    narrow(out, s, 1, WIDE, lambda q: ywrap[:, s, q:q + B * MC].rearrange("p (i m) -> p i m", i=B)[:, :, 0:MC:2])
                    ins = narrow(out[:, :, 15], s, 1, EDGED, lambda q: ywrap[:, s, (30 + q) % MC:B * MC:MC])
                ins.then_inc(prod, 1)

            def run(t, s, following, after):
                if following:
                    build(*following)
                for k in range(NB):
                    multiply(t, s, k)
            pe.wait_ge(clear, CLEARS)
            tasks(pe, build, run)

        bank = lambda k: (ps[:, PM + k].rearrange("p (n j) -> p n j", j=4) if k < 3 else
                          ps[:, PM + k].rearrange("p (j n) -> p n j", j=4))

        @block.scalar
        def _(act):
            def inputs(t, s):
                act.wait_ge(win_in[s], 64 * (t + 1))
                for r in range(2):
                    half = slice(64 * r, 64 * r + 64)
                    w = fwin[half, s]
                    src = bass.AP(w.tensor, w.offset, [list(w.ap[0]), [16, 8], [1, 8]])
                    act.copy(filt[half, s, half].rearrange("p (a b) -> p a b", a=8), src).then_inc(filt_set, 1)

            def columns(t, s):
                u = 2 * t + s
                act.wait_ge(built, u + 1)
                act.copy(cols[:, s], ps[:, PB, 0:NR * NCOL].rearrange("p (a b) -> p a b", b=NCOL)).then_inc(cols_set, 1)
                act.wait_ge(cols_set, u + 1)
                act.copy(cols2[:, s, 0], cols[:, s, 0:P8, 0:NIDX]).then_inc(cols_high, 1)

            def split(t, s, k):
                if k == 0:
                    act.wait_ge(d_in[s], 32 * (t + 1))
                act.copy(yt[0][:, s, k * QUART:(k + 1) * QUART], d[:, s, k].rearrange("p b m -> p (b m)")).then_inc(high_set, 1)
                if k == 2:
                    for r, row in ((0, BR - 1), (1, 0)):
                        act.copy(ywrap[64 * r:64 * r + 64, s, 0:B * MC].rearrange("p (i m) -> p i m", i=B), d[0:64, s, :, row]
                                 ).then_inc(wrap_set, 1)

            def prepare(t, s):
                columns(t, s)
                for k in range(4):
                    split(t, s, k)

            def run(t, s, following, after):
                u = 2 * t + s
                if following:
                    columns(*following)
                for k in range(NB):
                    if following and k < 4:
                        split(*following, k)
                    if after and k == 3:
                        inputs(*after)
                    if s == 0:
                        act.wait_ge(prod, NB * u + k + 1)
                        wait(act, gated, NB * t - 4 + k)
                        if k < 4:
                            act.activation(g1[:, k].rearrange("p (n j) -> p n j", j=4), bank(k), AF.Gelu).then_inc(gelu_set, 1)
                        else:
                            act.activation(g1w[:], ps[:, PM + 4, 0:64], AF.Gelu).then_inc(gelu_set, 1)
            act.wait_ge(clear, CLEARS)
            inputs(0, 0)
            inputs(0, 1)
            tasks(act, prepare, run)

        @block.vector
        def _(v):
            v.memset(filt[:], 0.0).then_inc(clear, 1)
            v.memset(win[:], 0.0).then_inc(clear, 1)
            v.memset(zero[:], 0.0).then_inc(clear, 1)
            v.memset(d[64:128, :, :, BR - 1], 0.0).then_inc(clear, 1)
            v.memset(ywrap[:], 0.0).then_inc(clear, 1)
            v.memset(mat[:], 0.0).then_inc(clear, 1)
            v.memset(mat2[:].bitcast(F32), 0.0).then_inc(clear, 1)
            v.wait_ge(clear, CLEARS)

            def inputs(t, s):
                v.wait_ge(win_in[s], 64 * (t + 1))
                for q, at in ((0, 9), (1, 3)):
                    v.scalar_tensor_tensor(edge[:, s, :, 2 * q:2 * q + 2], xwin[:, s, :, 2 * q:2 * q + 2], keep["xmask"][:, q:q + 1],
                                           win[:, s, :, at:at + 2], ALU.mult, ALU.add).then_inc(edge_set, 1)

            def columns(t, s):
                u = 2 * t + s
                v.wait_ge(cols_high, u + 1)
                v.tensor_tensor(cols2[:, s, 1], cols[:, s, 0:P8, 0:NIDX], cols2[:, s, 0].bitcast(F32), ALU.subtract
                                ).then_inc(cols_low, 1)

            def split(t, s, k):
                u = 2 * t + s
                part = slice(k * QUART, (k + 1) * QUART)
                v.wait_ge(high_set, 4 * u + k + 1)
                v.tensor_tensor(yt[1][:, s, part], d[:, s, k].rearrange("p b m -> p (b m)"), yt[0][:, s, part].bitcast(F32), ALU.subtract
                                ).then_inc(low_set, 1)
                if k == 2:
                    col = lambda m, n: d[:, s].rearrange("p i b m -> p m (i b)")[:, m:m + n]
                    v.tensor_copy(yedge[:, s, 0:2], col(MC - 2, 2)).then_inc(yedge_set, 1)
                    v.tensor_copy(yedge[:, s, 2:3], col(0, 1)).then_inc(yedge_set, 1)

            def prepare(t, s):
                columns(t, s)
                for k in range(4):
                    split(t, s, k)

            def run(t, s, following, after):
                u = 2 * t + s
                if following:
                    columns(*following)
                for k in range(NB):
                    if following and k < 4:
                        split(*following, k)
                    if after and k == 3:
                        inputs(*after)
                    if s == 1:
                        v.wait_ge(prod, NB * u + k + 1)
                        v.wait_ge(gelu_set, NB * t + k + 1)
                        if k == 0:
                            wait(v, g_out, 16 * t)
                        if k < 4:
                            v.scalar_tensor_tensor(gt[:, :, :, 4 * k:4 * k + 4].rearrange("p i b j -> p (i b) j"), bank(k), 0.0,
                                                   g1[:, k].rearrange("p (n j) -> p n j", j=4), ALU.max, ALU.mult).then_inc(gated, 1)
                        else:
                            v.wait_ge(gated, NB * t + 4)
                            rows = lambda a: a.rearrange("p (i j) -> p i j", i=B)
                            v.scalar_tensor_tensor(gt[:, :, BR - 1], rows(ps[:, PM + 4, 0:64]), 0.0, rows(g1w[:]),
                                                   ALU.max, ALU.mult).then_inc(gated, 1)
            inputs(0, 0)
            inputs(0, 1)
            tasks(v, prepare, run)

        @block.gpsimd
        def _(pool):
            def spread(t, s):
                pool.wait_ge(cols_low, 2 * t + s + 1)
                pool.tensor_tensor(held[:, s:s + 1], zero[:], zero[:], ALU.add)
                for kind, c0, c1, at in ((0, 0, 8, 6), (2, 2, 11, 0), (2, 11, 13, NIDX), (4, 13, 15, NIDX + 2), (4, 15, 16, 5)):
                    src = cols[:, s, :, at:at + c1 - c0].rearrange("p (r a) b -> p r a b", r=2)
                    pool.tensor_copy(mat[:, s, :, kind, :, c0:c1], src)
                for kind, q, c0, c1, at in ((1, 1, 2, 16, 0), (3, 2, 10, 16, 0)):
                    pool.tensor_copy(mat[:, s, 1, kind, :, c0:c1], cols[:, s, P8:, at:at + c1 - c0])
                for q, c0, c1, at in ((0, 0, 8, 6), (1, 2, 16, 0), (2, 10, 16, 0)):
                    ins = pool.tensor_copy(mat2[:, s, :, q, :, c0:c1], cols2[:, s, :, :, at:at + c1 - c0])
                ins.then_inc(mat_set, 1)

            def run(t, s, following, after):
                if following:
                    spread(*following)
            pool.wait_ge(clear, CLEARS)
            tasks(pool, spread, run)


def stage_d(nc, io, keep, scratch):
    NP = 16 * 512
    with ExitStack() as ctx:
        sb = lambda name, shape: ctx.enter_context(nc.sbuf_tensor(name, shape, F32))
        sem = lambda name: ctx.enter_context(nc.semaphore(name))
        ps = ctx.enter_context(nc.psum_tensor("psD", [128, 8, 512], F32))
        g = sb("g", [DIM, 2, 2, NP])
        xt = sb("xt", [DIM, 2, BR, W])
        g_in = [sem(f"gd_in{k}") for k in range(2)]
        x_in = [sem(f"xd_in{k}") for k in range(2)]
        rectified = sem("rectified")
        mm = sem("mm_d")
        added = sem("added")
        out_st = [sem(f"out_st{k}") for k in range(2)]
        block = ctx.enter_context(nc.Block())
        moves = lambda p: 16 if p < 5 else 32
        before = lambda p: sum(moves(q) for q in range(p % 2, p, 2))
        total = [before(8 + k) for k in range(2)]

        def rows(ap, img, p, slot):
            top = OFF + p
            full = BR if top < 8 else BR - 1
            yield dram(ap, img * (DIM * PIX) + top * W, [[PIX, DIM], [ROWPIX, full], [1, W]]), xt[:, slot, 0:full]
            if full < BR:
                yield dram(ap, img * (DIM * PIX) + (top - 8) * W, [[PIX, DIM], [1, W]]), xt[:, slot, BR - 1]

        def each(eng, strip):
            over(eng, B, lambda img: [strip(img, p, 8 * img + p, p % 2) for p in range(P8)])

        @block.sync
        def _(sp):
            def load(img, p, n, slot):
                wait(sp, mm, 16 * (n - 1))
                for kt in range(2):
                    sp.dma_start(g[:, slot, kt].rearrange("p (a b) -> p a b", b=512),
                                 dram(scratch["g"], kt * DIM * 128 * TILES + p * 16 * TILES + img * 512,
                                      [[128 * TILES, DIM], [TILES, 16], [1, 512]])).then_inc(g_in[slot], 16)
                wait(sp, out_st[slot], img * total[slot] + before(p))
                for far, near in rows(io["x"], img, p, slot):
                    sp.dma_start(near, far).then_inc(x_in[slot], 16)
            each(sp, load)

        @block.tensor
        def _(pe):
            def strip(img, p, n, slot):
                for c in range(16):
                    if c % 4 == 0:
                        pe.wait_ge(rectified, 4 * n + c // 4 + 1)
                    wait(pe, added, 16 * n + c - 7)
                    for kt in range(2):
                        ins = pe.matmul(ps[0:DIM, c % 8, :], keep["w_outT"][:, kt], g[:, slot, kt, c * 512:(c + 1) * 512],
                                        start=(kt == 0), stop=(kt == 1))
                    ins.then_inc(mm, 1)
            each(pe, strip)

        @block.vector
        def _(v):
            def strip(img, p, n, slot):
                v.wait_ge(x_in[slot], img * total[slot] + before(p) + moves(p))
                for c in range(16):
                    v.wait_ge(mm, 16 * n + c + 1)
                    nj = TJ if c < 13 else TJ - 1
                    add = ps[0:DIM, c % 8].rearrange("p (b j) -> p b j", j=TJ)
                    if nj < TJ:
                        dst = xt[:, slot, :, c - 13]
                        v.tensor_tensor(dst, add[:, :, nj], dst, ALU.add)
                    dst = xt[:, slot, :, OFF + c:OFF + c + 16 * (nj - 1) + 1:16]
                    v.tensor_tensor(dst, add[:, :, 0:nj], dst, ALU.add).then_inc(added, 1)
            each(v, strip)

        @block.scalar
        def _(act):
            def rectify(img, p):
                slot = p % 2
                act.wait_ge(g_in[slot], 32 * 4 * img + 32 * (p // 2 + 1))
                for q in range(4):
                    part = g[:, slot, :, q * (NP // 4):(q + 1) * (NP // 4)]
                    act.activation(part, part, AF.Relu).then_inc(rectified, 1)

            def image(img, last):
                for p in range(P8):
                    if p < P8 - 1:
                        rectify(img, p + 1)
                    elif not last:
                        rectify(img + 1, 0)
                    act.wait_ge(added, 16 * (8 * img + p + 1))
                    for far, near in rows(io["out"], img, p, p % 2):
                        act.dma_start(far, near).then_inc(out_st[p % 2], 16)
            rectify(0, 0)
            with act.Fori(0, B - 1) as img:
                image(img, False)
            image(B - 1, True)
            for k in range(2):
                act.wait_ge(out_st[k], B * total[k])


def build(nc, io):
    with ExitStack() as ctx:
        sb = lambda name, shape: ctx.enter_context(nc.sbuf_tensor(name, shape, F32))
        keep = {
            "ident": sb("ident", [128, 128]),
            "xmask": sb("xmask", [128, 2]),
            "w_inT": sb("w_inT", [DIM, C2]),
            "w_outT": sb("w_outT", [DIM, 2, DIM]),
            "scale": sb("scale", [DIM, B]),
            "shift": sb("shift", [DIM, B]),
        }
        scratch = {
            "kper": nc.dram_tensor("kper_d", [C2, KTAB], F32).ap(),
            "tab": nc.dram_tensor("tab_d", [C2, TAB], F32).ap(),
            "xtab": nc.dram_tensor("xtab_d", [C2, XTAB], F32).ap(),
            "y": [nc.dram_tensor(f"y{s}_d", [HID, B * PIX], F32).ap() for s in range(2)],
            "g": nc.dram_tensor("g_d", [HID, 128 * TILES], F32).ap(),
        }
        stage_a(nc, io, keep, scratch)
        stage_b(nc, io, keep, scratch)
        stage_c(nc, keep, scratch)
        stage_d(nc, io, keep, scratch)


def constants():
    import numpy as np
    ident = np.eye(128, dtype=np.float32)
    group = np.zeros((DIM, DIM), np.float32)
    for k in range(DIM):
        group[k, k // 3 * 3:k // 3 * 3 + 3] = 1.0 / 3
    u, v = np.meshgrid(np.arange(8), np.arange(5), indexing="ij")
    weight = np.where((v == 0) | (v == 4), 1.0, 2.0) / 64
    i, j = np.meshgrid(np.arange(15), np.arange(16), indexing="ij")
    dft = weight.reshape(40, 1) * np.cos(2 * np.pi * (u.reshape(40, 1) * (i.reshape(1, -1) - 7) + v.reshape(40, 1) * (j.reshape(1, -1) - 7)) / 8)
    col = 7 - np.arange(128) % 8
    xmask = -np.stack([col == 7, col == 0], 1).astype(np.float32)
    return {"ident": ident, "group": group, "dft": dft.astype(np.float32), "xmask": xmask}


_INS = {"x": "x", "w_in": "L0_conv_w_in", "w_dw": "L0_conv_w_dw", "w_dw3": "L0_conv_w_dw3", "w_dw5": "L0_conv_w_dw5",
        "filt": "L0_conv_fft_filt", "w_out": "L0_conv_w_out"}


def kernel(**inputs):
    import numpy as _np
    import concourse.bacc as _bacc
    from concourse import mybir as _mybir
    from concourse.bass_utils import run_bass_kernel_spmd as _run

    nc = _bacc.Bacc("TRN2", target_bir_lowering=False, num_devices=1)
    arrays, io = {}, {}
    for name, full in _INS.items():
        arrays[f"in_{name}"] = _np.ascontiguousarray(inputs[full])
    for name, value in constants().items():
        arrays[f"in_{name}"] = value
    for name, a in arrays.items():
        io[name[3:]] = nc.dram_tensor(name, a.shape, _mybir.dt.from_np(a.dtype), kind="ExternalInput").ap()
    io["out"] = nc.dram_tensor("out_0", (B, DIM, H, W), _mybir.dt.float32, kind="ExternalOutput").ap()
    build(nc, io)
    r = _run(nc, [arrays], core_ids=[0])
    return r.results[0]["out_0"]
```

```python
from contextlib import ExitStack

import concourse.bass as bass
from concourse import mybir

F32 = mybir.dt.float32
F32R = mybir.dt.float32r
ALU = mybir.AluOpType
AF = mybir.ActivationFunctionType

B, DIM, H, W = 4, 96, 256, 256
HID = 2 * DIM
C2 = 2 * HID
PIX = H * W
P8 = 8
BR = H // P8
MC = W // P8
TJ = W // 16
OFF = 3
ROWPIX = P8 * W
CT = C2 // 128
NIDX = 14
TROW = NIDX + 8
ZT = 16
TAB = ZT * 2 * P8 * TROW
WIN = (2 * P8 - 1) * TROW + NIDX
XTAB = ZT * 2 * P8 * 4
KTAB = 15 * 16
KWIN = 7 * 16 + 8
NE = 11
NCOL = NIDX + 4
TILES = B * BR * TJ
TILES2 = B * BR * MC
EPS = 1e-5
EDGE = [(0, 4), (0, 3), (2, 1), (2, 0)]


def wait(eng, sem, value):
    if not isinstance(value, int) or value > 0:
        eng.wait_ge(sem, value)


def over(eng, n, body):
    body(0)
    with eng.Fori(1, n) as i:
        body(i)


def dram(tensor, offset, dims):
    return bass.AP(tensor.tensor, offset, dims)


def stage_a(nc, io, keep, scratch):
    CH = 2048
    NCH = PIX // CH
    RING = 4
    with ExitStack() as ctx:
        sb = lambda name, shape: ctx.enter_context(nc.sbuf_tensor(name, shape, F32))
        sem = lambda name: ctx.enter_context(nc.semaphore(name))
        ps = ctx.enter_context(nc.psum_tensor("psA", [128, 8, 512], F32))
        xs = sb("xsA", [DIM, RING, CH])
        stats = sb("stats", [DIM, NCH * CH // 512, 6])
        mv = sb("mv", [DIM, B, 2])
        small = sb("small", [DIM, 10, B])
        win = sb("win", [128, CT, DIM])
        wout = sb("wout", [DIM, HID])
        filt = sb("filt", [128, CT, 40])
        filtT = sb("filtT", [40, C2])
        dft = sb("dft", [40, KTAB])
        group = sb("group", [DIM, DIM])
        kper = sb("kper", [128, CT, KTAB])
        w1 = sb("w1", [128, CT, 9])
        w2 = sb("w2", [128, CT, 25])
        prod = sb("prod", [128, CT, 3, 5])
        h = sb("h", [128, NE, CT, 3, 5])
        cf = sb("cf", [128, CT, 7, NE])
        tab = sb("tab", [128, CT, ZT, 2, P8, TROW])
        xtab = sb("xtab", [128, CT, ZT, 2, P8, 4])
        x_in = [sem(f"x_in{k}") for k in range(RING)]
        x_used = sem("x_used")
        params = sem("params")
        w2_clear = sem("w2_clear")
        w2_in = sem("w2_in")
        turned = sem("turned")
        turned_sb = sem("turned_sb")
        kper_ps = sem("kper_ps")
        kper_sb = sem("kper_sb")
        aggr = sem("aggr")
        seg = sem("seg")
        g_mean = sem("g_mean")
        g_in = sem("g_in")
        g_var = sem("g_var")
        var_eps = sem("var_eps")
        root = sem("root")
        vchain = sem("vchain")
        pchain = sem("pchain")
        tab_ready = sem("tab_ready")
        tab_out = sem("tab_out")
        kper_out = sem("kper_out")
        block = ctx.enter_context(nc.Block())

        @block.sync
        def _(sp):
            for dst, src in ((keep["ident"][:], io["ident"]), (keep["xmask"][:], io["xmask"]),
                             (dft[:], io["dft"]), (group[:], io["group"]), (wout[:], io["w_out"]),
                             (win[:], io["w_in"].rearrange("(t p) c -> p t c", p=128)),
                             (filt[:], io["filt"].rearrange("(t p) a b u v -> p t (a b u v)", p=128)),
                             (w1[:], io["w_dw"].rearrange("(t p) a u v -> p t (a u v)", p=128))):
                sp.dma_start(dst, src).then_inc(params, 16)
            sp.wait_ge(w2_clear, 1)
            w3 = io["w_dw3"].rearrange("o a u v -> o (a u) v")
            w5 = io["w_dw5"].rearrange("o a u v -> o (a u v)")
            mid = w2[:].rearrange("p t (u v) -> p t u v", u=5)[:, :, 1:4, 1:4]
            sp.dma_start(mid[:, 0], w3[0:128]).then_inc(w2_in, 16)
            sp.dma_start(mid[0:64, 1], w3[128:192]).then_inc(w2_in, 16)
            sp.dma_start(w2[64:128, 1], w5[0:64]).then_inc(w2_in, 16)
            sp.dma_start(w2[:, 2], w5[64:192]).then_inc(w2_in, 16)

            def load(img, q):
                for k in range(RING):
                    n = img * (NCH) + q * RING + k
                    wait(sp, x_used, n - (RING - 1))
                    sp.dma_start(xs[:, k], dram(io["x"], img * (DIM * PIX) + (q * RING + k) * CH, [[PIX, DIM], [1, CH]])
                                 ).then_inc(x_in[k], 16)
            for img in range(B):
                over(sp, NCH // RING, lambda q, img=img: load(img, q))

        @block.vector
        def _(v):
            def chain(ins):
                chain.n += 1
                ins.then_inc(vchain, 1)
                v.wait_ge(vchain, chain.n)
            chain.n = 0
            v.memset(w2[:], 0.0).then_inc(w2_clear, 1)

            def chunk_stats(img, q):
                for k in range(RING):
                    v.wait_ge(x_in[k], (img * (NCH // RING) + q + 1) * 16)
                    for j in range(CH // 512):
                        at = (q * RING + k) * (CH // 512) + j
                        ins = v.bn_stats(stats[:, at, :] if isinstance(at, int) else stats[:, bass.ds(at, 1), :],
                                         xs[:, k, j * 512:(j + 1) * 512])
                    ins.then_inc(x_used, 1)
            for img in range(B):
                if img:
                    v.wait_ge(aggr, img)
                over(v, NCH // RING, lambda q, img=img: chunk_stats(img, q))
                v.wait_ge(x_used, NCH * (img + 1))
                v.bn_aggr(mv[:, img, :], stats[:].rearrange("p a b -> p (a b)")).then_inc(aggr, 1)
            mg, dev, dv2, vin, ve, sd, r, t1, t2, t3 = (small[:, k, :] for k in range(10))
            v.wait_ge(g_mean, 1)
            chain(v.tensor_copy(mg, ps[0:DIM, 5, 0:B]))
            chain(v.tensor_tensor(dev, mv[:, :, 0], mg, ALU.subtract))
            chain(v.tensor_tensor(dv2, dev, dev, ALU.mult))
            v.tensor_tensor(vin, dv2, mv[:, :, 1], ALU.add).then_inc(g_in, 1)
            v.wait_ge(g_var, 1)
            v.tensor_scalar(ve, ps[0:DIM, 6, 0:B], EPS, None, ALU.add).then_inc(var_eps, 1)
            v.wait_ge(root, 1)
            chain(v.reciprocal(r, sd))
            v.wait_ge(var_eps, 1)
            chain(v.tensor_tensor(t1, r, r, ALU.mult))
            chain(v.tensor_tensor(t2, t1, ve, ALU.mult))
            chain(v.tensor_scalar(t3, t2, -0.5, 1.5, ALU.mult, ALU.add))
            chain(v.tensor_tensor(keep["scale"][:], r, t3, ALU.mult))
            chain(v.tensor_tensor(dev, mg, keep["scale"][:], ALU.mult))
            v.tensor_scalar(keep["shift"][:], dev, -1.0, None, ALU.mult)

        @block.tensor
        def _(pe):
            pe.wait_ge(params, 16 * 8)
            ident = keep["ident"]
            for t in range(CT):
                pe.transpose(ps[0:DIM, 0, t * 128:(t + 1) * 128], win[:, t, :], ident[:])
            for t in range(CT):
                pe.transpose(ps[0:40, 1, t * 128:(t + 1) * 128], filt[:, t, :], ident[:])
            for t in range(2):
                ins = pe.transpose(ps[0:DIM, 2, t * DIM:(t + 1) * DIM], wout[:, t * DIM:(t + 1) * DIM], ident[0:DIM, 0:DIM])
            ins.then_inc(turned, 1)
            pe.wait_ge(turned_sb, 1)
            for t in range(CT):
                ins = pe.matmul(ps[:, 3 + t // 2, (t % 2) * KTAB:(t % 2 + 1) * KTAB], filtT[:, t * 128:(t + 1) * 128], dft[:],
                                start=True, stop=True)
            ins.then_inc(kper_ps, 1)
            pe.wait_ge(aggr, B)
            pe.matmul(ps[0:DIM, 5, 0:B], group[:], mv[:, :, 0], start=True, stop=True).then_inc(g_mean, 1)
            pe.wait_ge(g_in, 1)
            pe.matmul(ps[0:DIM, 6, 0:B], group[:], small[:, 3, :], start=True, stop=True).then_inc(g_var, 1)

        @block.scalar
        def _(act):
            act.wait_ge(turned, 1)
            act.copy(filtT[:], ps[0:40, 1, 0:C2]).then_inc(turned_sb, 1)
            act.copy(keep["w_inT"][:], ps[0:DIM, 0, 0:C2])
            act.copy(keep["w_outT"][:].rearrange("p a b -> p (a b)"), ps[0:DIM, 2, 0:2 * DIM])
            act.wait_ge(kper_ps, 1)
            act.copy(kper[:, 0:2].rearrange("p a b -> p (a b)"), ps[:, 3, 0:2 * KTAB]).then_inc(kper_sb, 1)
            act.copy(kper[:, 2], ps[:, 4, 0:KTAB]).then_inc(kper_sb, 1)
            act.wait_ge(kper_sb, 2)
            act.dma_start(scratch["kper"].rearrange("(t p) k -> p t k", p=128), kper[:]).then_inc(kper_out, 16)
            act.wait_ge(tab_ready, 1)
            for t in range(CT):
                act.dma_start(scratch["tab"][t * 128:(t + 1) * 128], tab[:, t].rearrange("p a b c d -> p (a b c d)")).then_inc(tab_out, 16)
                act.dma_start(scratch["xtab"][t * 128:(t + 1) * 128], xtab[:, t].rearrange("p a b c d -> p (a b c d)")).then_inc(tab_out, 16)
            act.wait_ge(var_eps, 1)
            act.activation(small[:, 5, :], small[:, 4, :], AF.Sqrt).then_inc(root, 1)
            act.wait_ge(kper_out, 16)
            act.wait_ge(tab_out, 32 * CT)

        @block.gpsimd
        def _(pool):
            def chain(ins):
                chain.n += 1
                ins.then_inc(pchain, 1)
                pool.wait_ge(pchain, chain.n)
            chain.n = 0
            pool.memset(tab[:], 0.0)
            pool.memset(xtab[:], 0.0)
            chain(pool.memset(h[:], 0.0))
            pool.wait_ge(params, 16 * 8)
            pool.wait_ge(w2_in, 64)
            w1v = w1[:].rearrange("p t (a b) -> p t a b", a=3)
            w2v = w2[:].rearrange("p t (a b) -> p t a b", a=5)

            def rows_outer(ac, bc):
                chain(pool.tensor_tensor(prod[:], w1v[:, :, :, ac:ac + 1].broadcast_to([128, CT, 3, 5]),
                                         w2v[:, :, :, bc].unsqueeze(2).broadcast_to([128, CT, 3, 5]), ALU.mult))
            for ac in range(3):
                for bc in range(5):
                    rows_outer(ac, bc)
                    e = 6 - ac - bc
                    chain(pool.tensor_tensor(h[:, e], h[:, e], prod[:], ALU.add))
            for k, (ac, bc) in enumerate(EDGE):
                rows_outer(ac, bc)
                chain(pool.tensor_copy(h[:, 7 + k], prod[:]))
            chain(pool.memset(cf[:], 0.0))
            for a in range(3):
                for t in range(CT):
                    dst = cf[:, t, a:a + 5, :]
                    ins = pool.tensor_tensor(dst, dst, h[:, :, t, a, :].rearrange("p e b -> p b e"), ALU.add)
                chain(ins) if a == 2 else chain(ins)
            for z in range(ZT):
                zt = 7 - z if z < 8 else 23 - z
                for p in range(P8):
                    d = z - p
                    if not 0 <= d <= 6:
                        continue
                    for r in range(2):
                        if r == 1 and (z < 8) != (p + OFF < 8):
                            continue
                        pool.tensor_copy(tab[:, :, zt, r, p, 7:14], cf[:, :, d, 0:7])
                        ins = pool.tensor_copy(xtab[:, :, zt, r, p, :], cf[:, :, d, 7:NE])
            chain(ins)
            for z, p, a, b in ((7, 3, 0, 4), (7, 4, 0, 3), (8, 5, 2, 1), (8, 6, 2, 0)):
                zt = 7 - z if z < 8 else 23 - z
                for dst, e0, e1 in ((tab[:, :, zt, 1, p, 7:14], 0, 7), (xtab[:, :, zt, 1, p, :], 7, NE)):
                    ins = pool.tensor_tensor(dst, dst, h[:, e0:e1, :, a, b].rearrange("p e t -> p t e"), ALU.subtract)
            ins.then_inc(tab_ready, 1)


def stage_b(nc, io, keep, scratch):
    G = 4
    NG = BR // G
    NS = CT * G * 2
    by = lambda n: n % 3 == 2
    before = lambda n: sum(by(k) == by(n) for k in range(n))
    with ExitStack() as ctx:
        sb = lambda name, shape: ctx.enter_context(nc.sbuf_tensor(name, shape, F32))
        sem = lambda name: ctx.enter_context(nc.semaphore(name))
        ps = ctx.enter_context(nc.psum_tensor("psB", [128, 4, 1024], F32))
        xs = sb("xsB", [DIM, G, ROWPIX])
        xn = sb("xn", [DIM, 2, G, ROWPIX])
        y = sb("y", [128, CT, P8 * P8, G, MC])
        x_in = [sem(f"xb_in{k}") for k in range(G)]
        scaled = sem("scaled")
        normed = sem("normed")
        mm = sem("mm")
        copied = {False: sem("by_dve"), True: sem("by_act")}
        each_group = {e: sum(by(n) == e for n in range(NS)) for e in (False, True)}
        stored = [sem(f"y_stored{t}") for t in range(CT)]
        parts = ((0, 0, 128, 0, 0), (1, 0, 64, 0, 128), (1, 64, 128, 1, 0), (2, 0, 128, 1, 64))
        nparts = [sum(p[0] == t for p in parts) for t in range(CT)]
        CHS = B * PIX
        block = ctx.enter_context(nc.Block())

        def groups(eng, group):
            for img in range(B):
                over(eng, NG // 2, lambda i, img=img: [group(img, 2 * i + par, NG * img + 2 * i + par, par) for par in range(2)])

        @block.sync
        def _(sp):
            def load(img, q, g, par):
                for k in range(G):
                    wait(sp, normed, G * g + k - (G - 1))
                    sp.dma_start(xs[:, k], dram(io["x"], img * (DIM * PIX) + (q * G + k) * ROWPIX, [[PIX, DIM], [1, ROWPIX]])
                                 ).then_inc(x_in[k], 16)
            groups(sp, load)

        @block.gpsimd
        def _(pool):
            def norm(img, q, g, par):
                for k in range(G):
                    pool.wait_ge(x_in[k], g * 16 + 16)
                    if k == 0:
                        wait(pool, mm, NS * (g - 1))
                    pool.tensor_tensor(xn[:, par, k], xs[:, k], keep["scale"][:, img:img + 1].broadcast_to([DIM, ROWPIX]), ALU.mult
                                       ).then_inc(scaled, 1)
                    pool.wait_ge(scaled, G * g + k + 1)
                    pool.tensor_tensor(xn[:, par, k], xn[:, par, k], keep["shift"][:, img:img + 1].broadcast_to([DIM, ROWPIX]), ALU.add
                                       ).then_inc(normed, 1)
            groups(pool, norm)

        @block.tensor
        def _(pe):
            def group(img, q, g, par):
                for n in range(NS):
                    t, k, half = n // (2 * G), n // 2 % G, n % 2
                    if t == 0 and half == 0:
                        pe.wait_ge(normed, G * g + k + 1)
                    old, og = (n - 4, g) if n >= 4 else (n + NS - 4, g - 1)
                    if not (isinstance(og, int) and og < 0):
                        pe.wait_ge(copied[by(old)], each_group[by(old)] * og + before(old) + 1)
                    for c in range(2):
                        at = half * 1024 + c * 512
                        ins = pe.matmul(ps[:, n % 4, c * 512:(c + 1) * 512], keep["w_inT"][:, t * 128:(t + 1) * 128],
                                        xn[:, par, k, at:at + 512], start=True, stop=True)
                    ins.then_inc(mm, 1)
            groups(pe, group)

        def copy_out(eng, copy, me, img, q, g, par, ts):
            for n in range(NS):
                t, k, half = n // (2 * G), n // 2 % G, n % 2
                if by(n) != me or t not in ts:
                    continue
                if before(n) == 0 or n - 3 < t * 2 * G:
                    wait(eng, stored[t], 16 * nparts[t] * g)
                eng.wait_ge(mm, NS * g + n + 1)
                copy(y[:, t, 32 * half:32 * half + 32, k].rearrange("p (r c) m -> p r c m", r=4),
                     ps[:, n % 4].rearrange("p (r m c) -> p r c m", r=4, c=8)).then_inc(copied[me], 1)

        @block.vector
        def _(v):
            groups(v, lambda *a: copy_out(v, v.tensor_copy, False, *a, range(CT)))

        @block.scalar
        def _(act):
            def group(img, q, g, par):
                for t in range(CT):
                    copy_out(act, act.copy, True, img, q, g, par, (t,))
                    for e in (False, True):
                        last = max(n for n in range(2 * G * (t + 1)) if by(n) == e)
                        act.wait_ge(copied[e], each_group[e] * g + before(last) + 1)
                    for pt, p0, p1, half, c0 in parts:
                        if pt == t:
                            act.dma_start(dram(scratch["y"][half], c0 * CHS + img * (BR * MC) + q * (G * MC),
                                               [[CHS, p1 - p0], [TILES2, P8 * P8], [1, G * MC]]),
                                          y[p0:p1, t].rearrange("p a b c -> p a (b c)")).then_inc(stored[t], 16)
            groups(act, group)
            for t in range(CT):
                act.wait_ge(stored[t], 16 * nparts[t] * B * NG)


def stage_c(nc, keep, scratch):
    NB = 5
    NR = 2 * P8
    WIDE = (0, 1, 3)
    EDGED = (0, 2, 4)
    ORDER = (0, 1, 4, 2, 3)
    done = lambda k: ORDER.index(k) + 1
    PASSES = ((0, 0), (1, 0), (0, 1))
    QUART = TILES2 // 4
    with ExitStack() as ctx:
        sb = lambda name, shape, dt=F32: ctx.enter_context(nc.sbuf_tensor(name, shape, dt))
        sem = lambda name: ctx.enter_context(nc.semaphore(name))
        ps = ctx.enter_context(nc.psum_tensor("psC", [128, 8, 512], F32))
        PB, PM = 0, 1
        d = sb("d", [128, 2, B, BR, MC])
        yt = [sb(f"yt{k}", [128, 2, TILES2], F32R) for k in range(2)]
        ywrap = sb("ywrap", [128, 2, B * MC])
        yedge = sb("yedge", [128, 2, 2, B * BR])
        win = sb("win_c", [128, 2, NR, TROW])
        xwin = sb("xwin", [128, 2, NR, 4])
        fwin = sb("fwin", [128, 2, KWIN])
        filt = sb("filt_c", [128, 2, 128])
        cols = sb("cols", [128, 2, NR, NCOL])
        cols2 = sb("cols2", [128, 2, 2, P8, NIDX], F32R)
        mat = sb("mat", [128, 2, 2, 5, P8, 16])
        mat2 = sb("mat2", [128, 2, 2, 3, P8, 16], F32R)
        g1 = sb("g1", [128, 4, 512])
        g1w = sb("g1w", [128, 64])
        gt = sb("gt", [128, B, BR, TJ])
        zero = sb("zero", [128, 1])
        held = sb("held", [128, 2])
        d_in = [sem(f"d_in{s}") for s in range(2)]
        win_in = [sem(f"win_in{s}") for s in range(2)]
        shifted = [sem(f"shifted{k}") for k in range(B)]
        clear = sem("clear")
        high_set = sem("high_set")
        low_set = sem("low_set")
        wrap_in = [sem(f"wrap_in{s}") for s in range(2)]
        yedge_set = sem("yedge_set")
        edge_set = sem("edge_set")
        filt_set = sem("filt_set")
        built = sem("built")
        cols_set = sem("cols_set")
        cols_high = sem("cols_high")
        cols_low = sem("cols_low")
        mat_set = sem("mat_set")
        prod = sem("prod_c")
        gelu_set = sem("gelu_set")
        gated = sem("gated")
        g_out = sem("g_out")
        CHS = B * PIX
        CLEARS = 8
        block = ctx.enter_context(nc.Block())

        def shift(copy, t, s, k):
            copy(d[64:128, s, k, 0:BR - 1], d[0:64, s, k, 1:BR]).then_inc(shifted[k], 1)

        def tasks(eng, prepare, run):
            def pair(t, last=False):
                run(t, 0, (t, 1), None if last else (t + 1, 0))
                run(t, 1, None if last else (t + 1, 0), None if last else (t + 1, 1))
            prepare(0, 0)
            pair(0)
            with eng.Fori(1, HID - 1) as t:
                pair(t)
            pair(HID - 1, True)

        @block.sync
        def _(sp):
            sp.wait_ge(clear, CLEARS)

            def load(t, s):
                u = 2 * t + s
                ys = scratch["y"][s]
                wait(sp, built, u - 1)
                c = t + s * HID
                sp.dma_start(win[:, s].rearrange("p a b -> p (a b)")[:, 0:WIN],
                             dram(scratch["tab"], c * TAB, [[NR * TROW, ZT], [1, 8], [1, WIN]])).then_inc(win_in[s], 16)
                sp.dma_start(xwin[:, s].rearrange("p a b -> p (a b)"),
                             dram(scratch["xtab"], c * XTAB, [[64, ZT], [0, 8], [1, 64]])).then_inc(win_in[s], 16)
                for r in range(2):
                    sp.dma_start(fwin[64 * r:64 * r + 64, s],
                                 dram(scratch["kper"], c * KTAB, [[16, 8], [1, 8], [1, KWIN]])).then_inc(win_in[s], 16)
                wait(sp, low_set, 4 * (u - 1))
                sp.dma_start(d[0:64, s].rearrange("p i b m -> p (i b m)"),
                             dram(ys, t * CHS, [[TILES2, 64], [1, TILES2]])).then_inc(d_in[s], 16)

            def load_wrap(t, s):
                wait(sp, prod, NB * (2 * t + s - 1))
                for r, row in ((0, BR - 1), (1, 0)):
                    sp.dma_start(ywrap[64 * r:64 * r + 64, s, 0:B * MC].rearrange("p (i m) -> p i m", i=B),
                                 dram(scratch["y"][s], t * CHS + row * MC, [[TILES2, 64], [BR * MC, B], [1, MC]])).then_inc(wrap_in[s], 16)

            def store(t):
                sp.wait_ge(gated, NB * (t + 1))
                sp.dma_start(dram(scratch["g"], t * (128 * TILES), [[TILES, 128], [1, TILES]]),
                             gt[:].rearrange("p a b c -> p (a b c)")).then_inc(g_out, 16)

            load(0, 0)
            load_wrap(0, 0)
            load(0, 1)
            load_wrap(0, 1)
            load(1, 0)
            load(1, 1)
            load_wrap(1, 0)
            with sp.Fori(2, HID) as t:
                load(t, 0)
                load_wrap(t - 1, 1)
                store(t - 2)
                load(t, 1)
                load_wrap(t, 0)
            store(HID - 2)
            load_wrap(HID - 1, 1)
            store(HID - 1)
            sp.wait_ge(g_out, 16 * HID)

        @block.tensor
        def _(pe):
            def build(t, s):
                u = 2 * t + s
                pe.wait_ge(filt_set, 2 * (u + 1))
                pe.wait_ge(edge_set, 2 * (u + 1))
                wait(pe, cols_set, u)
                out = ps[:, PB, 0:NR * NCOL].rearrange("p (a b) -> p a b", b=NCOL)
                pe.matmul(out, filt[:, s], win[:, s, :, 0:NCOL], start=True, stop=True).then_inc(built, 1)

            def wide(out, s, src, columns=(0, 1, 2)):
                for q in columns:
                    for n, (pm, py) in enumerate(PASSES):
                        ins = pe.matmul(out, mat2[:, s, pm, q].rearrange("p a b -> p (a b)"), src(yt[py][:, s], q),
                                        start=(q == 0 and n == 0), stop=(q == 2 and n == 2))
                return ins

            def narrow(out, s, row, kinds, src, columns=(1, 2), last=False):
                for q in columns:
                    ins = pe.matmul(out, mat[:, s, row, kinds[q]].rearrange("p a b -> p (a b)"), src(q), start=(q == 0), stop=(last and q == 2))
                return ins

            def multiply(t, s, k):
                u = 2 * t + s
                if k == 0:
                    pe.wait_ge(low_set, 4 * (u + 1))
                    pe.wait_ge(yedge_set, 2 * (u + 1))
                    pe.wait_ge(mat_set, u + 1)
                if k == 4:
                    pe.wait_ge(wrap_in[s], 32 * (t + 1))
                if s == 0:
                    wait(pe, gated, NB * t - 4 + k)
                else:
                    pe.wait_ge(gelu_set, NB * t + done(k))
                if k < 3:
                    ins = wide(ps[:, PM + k].rearrange("p (i b j) -> p i b j", i=B, j=4)[:, :, 0:BR - 1], s, lambda y, q:
                               y.rearrange("p (i b m) -> p i b m", i=B, m=MC)[:, :, 0:BR - 1, 8 * k + q:8 * k + q + 7:2])
                elif k == 3:
                    out = ps[:, PM + 3].rearrange("p (j n) -> p j n", j=4)
                    src = lambda y, q: y.rearrange("p (n m) -> p m n", m=MC)[:, 24 + q:32:2]
                    wide(out, s, src, (0,))
                    narrow(out[:, 3], s, 0, EDGED, lambda q: yedge[:, s, q - 1])
                    ins = wide(out[:, 0:3], s, lambda y, q: src(y, q)[:, 0:3], (1, 2))
                else:
                    out = ps[:, PM + 4, 0:64].rearrange("p (i j) -> p i j", i=B)
                    src = lambda q, n: ywrap[:, s, 0:B * MC].rearrange("p (i m) -> p i m", i=B)[:, :, q:q + 2 * n - 1:2]
                    narrow(out, s, 1, WIDE, lambda q: src(q, TJ), (0,))
                    narrow(out[:, :, 0:TJ - 1], s, 1, WIDE, lambda q: src(q, TJ - 1))
                    ins = narrow(out[:, :, TJ - 1], s, 1, EDGED, lambda q: ywrap[:, s, (30 + q) % MC:B * MC:MC], last=True)
                ins.then_inc(prod, 1)

            def run(t, s, following, after):
                for k in ORDER:
                    multiply(t, s, k)
                    if k == 0 and following:
                        build(*following)
            pe.wait_ge(clear, CLEARS)
            tasks(pe, build, run)

        bank = lambda k: (ps[:, PM + k].rearrange("p (n j) -> p n j", j=4) if k < 3 else
                          ps[:, PM + k].rearrange("p (j n) -> p n j", j=4))

        @block.scalar
        def _(act):
            def inputs(t, s):
                act.wait_ge(win_in[s], 64 * (t + 1))
                for r in range(2):
                    half = slice(64 * r, 64 * r + 64)
                    w = fwin[half, s]
                    src = bass.AP(w.tensor, w.offset, [list(w.ap[0]), [16, 8], [1, 8]])
                    act.copy(filt[half, s, half].rearrange("p (a b) -> p a b", a=8), src).then_inc(filt_set, 1)

            def ahead(t, s, k):
                act.wait_ge(d_in[s], 16 * (t + 1))
                shift(act.copy, t, s, k)

            def columns(t, s):
                u = 2 * t + s
                act.wait_ge(built, u + 1)
                act.copy(cols[:, s], ps[:, PB, 0:NR * NCOL].rearrange("p (a b) -> p a b", b=NCOL)).then_inc(cols_set, 1)
                act.wait_ge(cols_set, u + 1)
                act.copy(cols2[:, s, 0], cols[:, s, 0:P8, 0:NIDX]).then_inc(cols_high, 1)

            def split(t, s, k):
                act.wait_ge(shifted[k], 2 * t + s + 1)
                act.copy(yt[0][:, s, k * QUART:(k + 1) * QUART], d[:, s, k].rearrange("p b m -> p (b m)")).then_inc(high_set, 1)

            def prepare(t, s):
                columns(t, s)
                for k in range(4):
                    split(t, s, k)

            def run(t, s, following, after):
                u = 2 * t + s
                for n, k in enumerate(ORDER):
                    if following and n == 0:
                        wait(act, prod, NB * u)
                    if following and n < 4:
                        split(*following, n)
                    if following and n == 0:
                        columns(*following)
                    if after and n == 3:
                        inputs(*after)
                        ahead(*after, 0)
                    if after and n == 4:
                        ahead(*after, 3)
                    if s == 0:
                        act.wait_ge(prod, NB * u + done(k))
                        wait(act, gated, NB * t - 4 + k)
                        if k < 4:
                            act.activation(g1[:, k].rearrange("p (n j) -> p n j", j=4), bank(k), AF.Gelu).then_inc(gelu_set, 1)
                        else:
                            act.activation(g1w[:], ps[:, PM + 4, 0:64], AF.Gelu).then_inc(gelu_set, 1)
            act.wait_ge(clear, CLEARS)
            for s in range(2):
                inputs(0, s)
                ahead(0, s, 0)
                ahead(0, s, 3)
            tasks(act, prepare, run)

        @block.vector
        def _(v):
            v.memset(filt[:], 0.0).then_inc(clear, 1)
            v.memset(win[:], 0.0).then_inc(clear, 1)
            v.memset(zero[:], 0.0).then_inc(clear, 1)
            v.memset(ps[:, PM:PM + 3], 0.0).then_inc(clear, 1)
            v.memset(d[64:128, :, :, BR - 1], 0.0).then_inc(clear, 1)
            v.memset(ywrap[:], 0.0).then_inc(clear, 1)
            v.memset(mat[:], 0.0).then_inc(clear, 1)
            v.memset(mat2[:].bitcast(F32), 0.0).then_inc(clear, 1)
            v.wait_ge(clear, CLEARS)

            def inputs(t, s):
                v.wait_ge(win_in[s], 64 * (t + 1))
                for q, at in ((0, 9), (1, 3)):
                    v.scalar_tensor_tensor(win[:, s, :, NIDX + 2 * q:NIDX + 2 * q + 2], xwin[:, s, :, 2 * q:2 * q + 2], keep["xmask"][:, q:q + 1],
                                           win[:, s, :, at:at + 2], ALU.mult, ALU.add).then_inc(edge_set, 1)

            def ahead(t, s):
                v.wait_ge(d_in[s], 16 * (t + 1))
                shift(v.tensor_copy, t, s, 1)

            def columns(t, s):
                u = 2 * t + s
                v.wait_ge(cols_high, u + 1)
                v.tensor_tensor(cols2[:, s, 1], cols[:, s, 0:P8, 0:NIDX], cols2[:, s, 0].bitcast(F32), ALU.subtract
                                ).then_inc(cols_low, 1)

            def split(t, s, k):
                u = 2 * t + s
                part = slice(k * QUART, (k + 1) * QUART)
                v.wait_ge(high_set, 4 * u + k + 1)
                if k == 3:
                    col = lambda m, n: d[:, s].rearrange("p i b m -> p m (i b)")[:, m:m + n]
                    v.tensor_copy(yedge[:, s, 0:1], col(MC - 1, 1)).then_inc(yedge_set, 1)
                    v.tensor_copy(yedge[:, s, 1:2], col(0, 1)).then_inc(yedge_set, 1)
                v.tensor_tensor(yt[1][:, s, part], d[:, s, k].rearrange("p b m -> p (b m)"), yt[0][:, s, part].bitcast(F32), ALU.subtract
                                ).then_inc(low_set, 1)

            def prepare(t, s):
                columns(t, s)
                for k in range(4):
                    split(t, s, k)

            def gate(t, k):
                v.wait_ge(prod, NB * (2 * t + 1) + done(k))
                v.wait_ge(gelu_set, NB * t + done(k))
                if k == 0:
                    wait(v, g_out, 16 * t)
                if k < 4:
                    v.scalar_tensor_tensor(gt[:, :, :, 4 * k:4 * k + 4].rearrange("p i b j -> p (i b) j"), bank(k), 0.0,
                                           g1[:, k].rearrange("p (n j) -> p n j", j=4), ALU.max, ALU.mult).then_inc(gated, 1)
                else:
                    v.wait_ge(gated, NB * t + 4)
                    rows = lambda a: a.rearrange("p (i j) -> p i j", i=B)
                    v.scalar_tensor_tensor(gt[:, :, BR - 1], rows(ps[:, PM + 4, 0:64]), 0.0, rows(g1w[:]),
                                           ALU.max, ALU.mult).then_inc(gated, 1)

            def run(t, s, following, after):
                for k in range(NB):
                    if following and k < 4:
                        split(*following, k)
                    if following and k == 0:
                        columns(*following)
                    if after and k == 3:
                        inputs(*after)
                    if after and k == 4:
                        ahead(*after)
                    if s == 1 and k > 1:
                        gate(t, k - 2)
                if s == 1:
                    gate(t, 3)
                    gate(t, 4)
            for s in range(2):
                inputs(0, s)
                ahead(0, s)
            tasks(v, prepare, run)

        @block.gpsimd
        def _(pool):
            def spread(t, s):
                pool.wait_ge(shifted[2], 2 * t + s + 1)
                pool.wait_ge(cols_low, 2 * t + s + 1)
                pool.tensor_tensor(held[:, s:s + 1], zero[:], zero[:], ALU.add)
                for kind, c0, c1, at in ((0, 0, 8, 6), (2, 2, 11, 0), (2, 11, 13, NIDX), (4, 13, 15, NIDX + 2), (4, 15, 16, 5)):
                    src = cols[:, s, :, at:at + c1 - c0].rearrange("p (r a) b -> p r a b", r=2)
                    pool.tensor_copy(mat[:, s, :, kind, :, c0:c1], src)
                for kind, q, c0, c1, at in ((1, 1, 2, 16, 0), (3, 2, 10, 16, 0)):
                    pool.tensor_copy(mat[:, s, 1, kind, :, c0:c1], cols[:, s, P8:, at:at + c1 - c0])
                for q, c0, c1, at in ((0, 0, 8, 6), (1, 2, 16, 0), (2, 10, 16, 0)):
                    ins = pool.tensor_copy(mat2[:, s, :, q, :, c0:c1], cols2[:, s, :, :, at:at + c1 - c0])
                ins.then_inc(mat_set, 1)

            def ahead(t, s):
                wait(pool, mat_set, 2 * t + s)
                pool.wait_ge(d_in[s], 16 * (t + 1))
                shift(lambda dst, src: pool.tensor_tensor(dst, src, zero[0:64, 0:1].unsqueeze(2).broadcast_to([64, BR - 1, MC]), ALU.add), t, s, 2)

            def run(t, s, following, after):
                if following:
                    spread(*following)
                if after:
                    ahead(*after)
            pool.wait_ge(clear, CLEARS)
            ahead(0, 0)


            def prepare(t, s):
                spread(t, s)
                ahead(t, 1)
            tasks(pool, prepare, run)


def stage_d(nc, io, keep, scratch):
    NP = 16 * 512
    with ExitStack() as ctx:
        sb = lambda name, shape: ctx.enter_context(nc.sbuf_tensor(name, shape, F32))
        sem = lambda name: ctx.enter_context(nc.semaphore(name))
        ps = ctx.enter_context(nc.psum_tensor("psD", [128, 8, 512], F32))
        g = sb("g", [DIM, 2, 2, NP])
        xt = sb("xt", [DIM, 2, BR, W])
        g_in = [sem(f"gd_in{k}") for k in range(2)]
        x_in = [sem(f"xd_in{k}") for k in range(2)]
        rectified = sem("rectified")
        mm = sem("mm_d")
        added = sem("added")
        out_st = [sem(f"out_st{k}") for k in range(2)]
        block = ctx.enter_context(nc.Block())
        moves = lambda p: 16 if p < 5 else 32
        before = lambda p: sum(moves(q) for q in range(p % 2, p, 2))
        total = [before(8 + k) for k in range(2)]

        def rows(ap, img, p, slot):
            top = OFF + p
            full = BR if top < 8 else BR - 1
            yield dram(ap, img * (DIM * PIX) + top * W, [[PIX, DIM], [ROWPIX, full], [1, W]]), xt[:, slot, 0:full]
            if full < BR:
                yield dram(ap, img * (DIM * PIX) + (top - 8) * W, [[PIX, DIM], [1, W]]), xt[:, slot, BR - 1]

        def each(eng, strip):
            over(eng, B, lambda img: [strip(img, p, 8 * img + p, p % 2) for p in range(P8)])

        @block.sync
        def _(sp):
            def load(img, p, n, slot):
                wait(sp, mm, 16 * (n - 1))
                for kt in range(2):
                    sp.dma_start(g[:, slot, kt].rearrange("p (a b) -> p a b", b=512),
                                 dram(scratch["g"], kt * DIM * 128 * TILES + p * 16 * TILES + img * 512,
                                      [[128 * TILES, DIM], [TILES, 16], [1, 512]])).then_inc(g_in[slot], 16)
                wait(sp, out_st[slot], img * total[slot] + before(p))
                for far, near in rows(io["x"], img, p, slot):
                    sp.dma_start(near, far).then_inc(x_in[slot], 16)
            each(sp, load)

        @block.tensor
        def _(pe):
            def strip(img, p, n, slot):
                for c in range(16):
                    if c % 4 == 0:
                        pe.wait_ge(rectified, 4 * n + c // 4 + 1)
                    wait(pe, added, 16 * n + c - 7)
                    for kt in range(2):
                        ins = pe.matmul(ps[0:DIM, c % 8, :], keep["w_outT"][:, kt], g[:, slot, kt, c * 512:(c + 1) * 512],
                                        start=(kt == 0), stop=(kt == 1))
                    ins.then_inc(mm, 1)
            each(pe, strip)

        @block.vector
        def _(v):
            def strip(img, p, n, slot):
                v.wait_ge(x_in[slot], img * total[slot] + before(p) + moves(p))
                for c in range(16):
                    v.wait_ge(mm, 16 * n + c + 1)
                    nj = TJ if c < 13 else TJ - 1
                    add = ps[0:DIM, c % 8].rearrange("p (b j) -> p b j", j=TJ)
                    if nj < TJ:
                        dst = xt[:, slot, :, c - 13]
                        v.tensor_tensor(dst, add[:, :, nj], dst, ALU.add)
                    dst = xt[:, slot, :, OFF + c:OFF + c + 16 * (nj - 1) + 1:16]
                    v.tensor_tensor(dst, add[:, :, 0:nj], dst, ALU.add).then_inc(added, 1)
            each(v, strip)

        @block.scalar
        def _(act):
            def rectify(img, p):
                slot = p % 2
                act.wait_ge(g_in[slot], 32 * 4 * img + 32 * (p // 2 + 1))
                for q in range(4):
                    part = g[:, slot, :, q * (NP // 4):(q + 1) * (NP // 4)]
                    act.activation(part, part, AF.Relu).then_inc(rectified, 1)

            def image(img, last):
                for p in range(P8):
                    if p < P8 - 1:
                        rectify(img, p + 1)
                    elif not last:
                        rectify(img + 1, 0)
                    act.wait_ge(added, 16 * (8 * img + p + 1))
                    for far, near in rows(io["out"], img, p, p % 2):
                        act.dma_start(far, near).then_inc(out_st[p % 2], 16)
            rectify(0, 0)
            with act.Fori(0, B - 1) as img:
                image(img, False)
            image(B - 1, True)
            for k in range(2):
                act.wait_ge(out_st[k], B * total[k])


def build(nc, io):
    with ExitStack() as ctx:
        sb = lambda name, shape: ctx.enter_context(nc.sbuf_tensor(name, shape, F32))
        keep = {
            "ident": sb("ident", [128, 128]),
            "xmask": sb("xmask", [128, 2]),
            "w_inT": sb("w_inT", [DIM, C2]),
            "w_outT": sb("w_outT", [DIM, 2, DIM]),
            "scale": sb("scale", [DIM, B]),
            "shift": sb("shift", [DIM, B]),
        }
        scratch = {
            "kper": nc.dram_tensor("kper_d", [C2, KTAB], F32).ap(),
            "tab": nc.dram_tensor("tab_d", [C2, TAB], F32).ap(),
            "xtab": nc.dram_tensor("xtab_d", [C2, XTAB], F32).ap(),
            "y": [nc.dram_tensor(f"y{s}_d", [HID, B * PIX], F32).ap() for s in range(2)],
            "g": nc.dram_tensor("g_d", [HID, 128 * TILES], F32).ap(),
        }
        stage_a(nc, io, keep, scratch)
        stage_b(nc, io, keep, scratch)
        stage_c(nc, keep, scratch)
        stage_d(nc, io, keep, scratch)


def constants():
    import numpy as np
    ident = np.eye(128, dtype=np.float32)
    group = np.zeros((DIM, DIM), np.float32)
    for k in range(DIM):
        group[k, k // 3 * 3:k // 3 * 3 + 3] = 1.0 / 3
    u, v = np.meshgrid(np.arange(8), np.arange(5), indexing="ij")
    weight = np.where((v == 0) | (v == 4), 1.0, 2.0) / 64
    i, j = np.meshgrid(np.arange(15), np.arange(16), indexing="ij")
    dft = weight.reshape(40, 1) * np.cos(2 * np.pi * (u.reshape(40, 1) * (i.reshape(1, -1) - 7) + v.reshape(40, 1) * (j.reshape(1, -1) - 7)) / 8)
    col = 7 - np.arange(128) % 8
    xmask = -np.stack([col == 7, col == 0], 1).astype(np.float32)
    return {"ident": ident, "group": group, "dft": dft.astype(np.float32), "xmask": xmask}


_INS = {"x": "x", "w_in": "L0_conv_w_in", "w_dw": "L0_conv_w_dw", "w_dw3": "L0_conv_w_dw3", "w_dw5": "L0_conv_w_dw5",
        "filt": "L0_conv_fft_filt", "w_out": "L0_conv_w_out"}


def kernel(**inputs):
    import numpy as _np
    import concourse.bacc as _bacc
    from concourse import mybir as _mybir
    from concourse.bass_utils import run_bass_kernel_spmd as _run

    nc = _bacc.Bacc("TRN2", target_bir_lowering=False, num_devices=1)
    arrays, io = {}, {}
    for name, full in _INS.items():
        arrays[f"in_{name}"] = _np.ascontiguousarray(inputs[full])
    for name, value in constants().items():
        arrays[f"in_{name}"] = value
    for name, a in arrays.items():
        io[name[3:]] = nc.dram_tensor(name, a.shape, _mybir.dt.from_np(a.dtype), kind="ExternalInput").ap()
    io["out"] = nc.dram_tensor("out_0", (B, DIM, H, W), _mybir.dt.float32, kind="ExternalOutput").ap()
    build(nc, io)
    r = _run(nc, [arrays], core_ids=[0])
    return r.results[0]["out_0"]
```
